# Optimizing a Trainium2 kernel written in Bass

```python
import numpy as np
import jax
import jax.numpy as jnp

def _softmax(x, axis=-1):
    return jax.nn.softmax(x, axis=axis)

def _gelu(x):
    return jax.nn.gelu(x, approximate=True)

def _silu(x):
    return jax.nn.silu(x)

def _sigmoid(x):
    return jax.nn.sigmoid(x)

def _layernorm(x, axis=-1, eps=1e-05):
    m = jnp.mean(x, axis=axis, keepdims=True)
    v = jnp.var(x, axis=axis, keepdims=True)
    return (x - m) / jnp.sqrt(v + eps)

def _scatter_add(tgt, idx, src, axis=0):
    return tgt.at[idx].add(src)

def _segment_sum(src, seg, n):
    return jax.ops.segment_sum(src, seg, n)
kernel_name = 'mk_adj_resnorm_d1_adj_r2_6aa61f'

def setup_inputs(seed: int=0):
    np.random.seed(seed)
    _w = jnp.asarray

    def _rec_inputs():
        import jax
        import jax.numpy as jnp
        _gk = jax.random.key(seed)
        x = -0.0004776 + 1.001 * jax.random.normal(jax.random.fold_in(_gk, 1), (2048, 512), jnp.float32)
        _w = (1.0 + jnp.arange(2048, dtype=jnp.float32)) ** (-0.5)
        _w = _w / _w.mean()
        _pij = jnp.clip(0.000976562 * _w[:, None] * _w[None, :], 0.0, 1.0)
        _a = jax.random.uniform(jax.random.fold_in(_gk, 2), (2048, 2048)) < _pij
        _a = jnp.logical_or(_a, jnp.eye(2048, dtype=bool))
        _af = _a.astype(jnp.float32)
        adj = _af
        return (x, adj)
    x, adj = _rec_inputs()

    def _L0_gnn_setup():
        import jax, jax.numpy as jnp
        import numpy as np
        N, H, E, HEADS = (1500, 512, 10000, 8)
        DK = H // HEADS
        key = jax.random.key(seed)
        k1, k2, k3, k4 = jax.random.split(key, 4)
        inst_feature = jax.random.normal(k1, (N, H), dtype=jnp.float32)
        rel_pair_index = jax.random.randint(k2, (E, 2), 0, N, dtype=jnp.int64)
        agg = jnp.zeros((N, N), dtype=jnp.float32)
        agg = agg.at[rel_pair_index[:, 0], rel_pair_index[:, 1]].set(1.0)
        agg = agg.at[jnp.arange(N), jnp.arange(N)].set(1.0)
        std = float(np.sqrt(2.0 / (H + DK)))
        Wq = jax.random.normal(k3, (H, H), dtype=jnp.float32) * std
        Wk = jax.random.normal(k4, (H, H), dtype=jnp.float32) * std
        bq = jnp.zeros((H,), dtype=jnp.float32)
        bk = jnp.zeros((H,), dtype=jnp.float32)
        return {'inst_feature': inst_feature, 'aggregator_matrix': agg, 'rel_pair_index': rel_pair_index, 'Wq': Wq, 'bq': bq, 'Wk': Wk, 'bk': bk}
    _L0_gnn_all = _L0_gnn_setup()
    _L0_gnn_in = {k: v for k, v in _L0_gnn_all.items() if k in ('rel_pair_index', 'Wq', 'bq', 'Wk', 'bk')}
    del _L0_gnn_all
    return {'x': x, 'adj': adj, 'L0_gnn_rel_pair_index': _L0_gnn_in['rel_pair_index'], 'L0_gnn_Wq': _L0_gnn_in['Wq'], 'L0_gnn_bq': _L0_gnn_in['bq'], 'L0_gnn_Wk': _L0_gnn_in['Wk'], 'L0_gnn_bk': _L0_gnn_in['bk']}

def reference(x, adj, L0_gnn_rel_pair_index, L0_gnn_Wq, L0_gnn_bq, L0_gnn_Wk, L0_gnn_bk):
    import jax
    import jax.numpy as jnp

    def _L0_gnn_ref(inst_feature, aggregator_matrix, rel_pair_index, Wq, bq, Wk, bk):
        import jax, jax.numpy as jnp
        import numpy as np
        N, H, E, HEADS = (1500, 512, 10000, 8)
        DK = H // HEADS
        n = inst_feature.shape[0]
        sub = rel_pair_index[:, 0]
        obj = rel_pair_index[:, 1]
        q = (inst_feature[sub] @ Wq.T + bq).reshape(-1, HEADS, DK)
        k = (inst_feature[obj] @ Wk.T + bk).reshape(-1, HEADS, DK)
        att = ((q * k).sum(-1) / np.sqrt(DK)).T.astype(inst_feature.dtype)
        scores = jnp.zeros((HEADS, n, n), dtype=inst_feature.dtype)
        scores = scores.at[:, sub, obj].set(att)
        mask = (1.0 - aggregator_matrix).astype(bool)
        scores = jnp.where(mask[None], -jnp.inf, scores)
        di = jnp.arange(n)
        scores = scores.at[:, di, di].set(1e-07)
        attn = jax.nn.softmax(scores, axis=2)
        aggregator_factor = attn.sum(axis=0) / HEADS
        return aggregator_factor @ inst_feature
    x = _layernorm(x + _L0_gnn_ref(x, adj, L0_gnn_rel_pair_index, L0_gnn_Wq, L0_gnn_bq, L0_gnn_Wk, L0_gnn_bk), axis=-1)
    return x

_drawn_inputs = setup_inputs


def setup_inputs(seed=0):
    import zlib

    import numpy as np

    out = dict(_drawn_inputs(seed))
    spreads = {'L0_gnn_bq': (0.0, 2.0), 'L0_gnn_bk': (0.0, 2.0)}
    factors = {'L0_gnn_Wq': 37.211, 'L0_gnn_Wk': 39.176}
    for name, (base, spread) in spreads.items():
        noise = np.random.default_rng([zlib.crc32(name.encode()), seed]).standard_normal(out[name].shape)
        drawn = base * np.exp(spread * noise) if base else spread * noise
        out[name] = jnp.asarray(drawn.astype(out[name].dtype))
    for name, factor in factors.items():
        out[name] = (out[name] * factor).astype(out[name].dtype)
    return out
```

```python
import concourse.bass as bass
from concourse import mybir
from contextlib import ExitStack
from collections import namedtuple


def graph_attention_norm(nc, x, adj, adj_blocks, adj_diag, edges, wq_t, bq, wk_t, bk, out):
    f32, f32r = mybir.dt.float32, mybir.dt.float32r
    bf16, i32, u32 = mybir.dt.bfloat16, mybir.dt.int32, mybir.dt.uint32
    ALU, ACT, AX = mybir.AluOpType, mybir.ActivationFunctionType, mybir.AxisListType

    N, H = x.shape
    E = edges.shape[0]
    HEADS = 8
    DK = H // HEADS
    P = 128
    T = N // P
    KC = H // P
    EP = 125
    EC = E // EP
    FIRST = 4
    ROUNDS = [1, 1] + [2] * ((T - 2) // 2)
    STARTS = [sum(ROUNDS[:r]) for r in range(len(ROUNDS))]
    NR = len(ROUNDS)
    SUMMED = T - 2
    SAVED = T - 4
    DIAG_SCORE = 1e-7
    BIG = 3.0e38
    EPS = 1e-5
    NT = -(-E // P)
    OC = 10
    NOC = EC // OC
    LOTS = 4
    LC = EC // LOTS
    GROUPS = [(0, 4), (4, 8), (8, 12), (12, 14), (14, 16)]

    ctx = ExitStack()
    with ctx:
        def sb(name, shape, dt):
            return ctx.enter_context(nc.sbuf_tensor(name, shape, dt))

        def pb(name, shape):
            return ctx.enter_context(nc.psum_tensor(name, shape, f32))

        def sems(prefix, names):
            return namedtuple("Semaphores", names)(*[ctx.enter_context(nc.semaphore(prefix + n)) for n in names.split()])

        sem = sems("", """x_r0 x_r1 x_r2 x_r3 x_r4 x_r5 x_r6 x_r7 x_r8 a_first_even a_first_odd a_even a_odd
            edges_in diag_in weights_in bq_in bk_in adj_lot0 adj_lot1 adj_lot2 adj_lot3 out_done
            x_high x_low masks_made products product_saved column_sums
            edge_index edge_split edge_values edge_distinct const_vector const_pool const_eye
            live scan totals prefix prefix_copied live_count ranks counts counts_copied
            row_table row_max row_e0 row_ed diag_flag zero_count den_a den_b den_c row_r
            w_terms d_terms w_sum d_sum w_done w_diag d_coef row_pack corr
            weighted x_scaled x_scaled_act base y_sum stats aggr std rstd shift y_done""")
        slot_steps = """onehot_made onehot_used slots slots_copied slot_ids slot_index slot_sub slot_key
            x_sub x_obj sub_turned obj_turned sub_turned_sbuf obj_turned_sbuf
            q_done k_done q_sbuf qk_product qk_sum att"""
        pair_steps = """id_rows other_row id_flags flag_max att_rows_a att_rows_b masked_a masked_b score_max"""
        value_steps = """keep edge_max centred exps rowvals sub_tiles row_onehot table"""
        spread_steps = """row_onehot_t gathered coef_terms coef_sum coef_diff coef cx cx_high cx_low"""
        one = sems("one_", slot_steps + " " + pair_steps + " " + value_steps + " " + spread_steps)
        gen = sems("gen_", "prepared first_slot slot_shift stored")
        gpair = sems("pair_", "column_loaded row_loaded offset mask flag_join score_join valid_loaded kept")
        gval = sems("val_", "loaded table_added")
        gout = sems("spread_", spread_steps + " loaded id_rows x_obj corr corr_added")
        x_r = [sem.x_r0, sem.x_r1, sem.x_r2, sem.x_r3, sem.x_r4, sem.x_r5, sem.x_r6, sem.x_r7, sem.x_r8]
        a_first = [sem.a_first_even, sem.a_first_odd]
        adj_lot = [sem.adj_lot0, sem.adj_lot1, sem.adj_lot2, sem.adj_lot3]
        a_par = [sem.a_even, sem.a_odd]

        xs = sb("xs", [P, T, H], f32)
        high_at = nc.sbuf_base
        xh = sb("xh", [P, T, H], f32r)
        xl = sb("xl", [P, T, H], f32r)
        prod = sb("prod", [P, SAVED, H], f32)
        blocks_at = nc.sbuf_base
        a = sb("a", [P, 2, N], f32)
        m_last = nc.alloc_sbuf_tensor_at("m_last", [P, N], f32r, offset=blocks_at + 4 * N)
        m = sb("m", [P, 3, N], f32r)
        weights_at = nc.sbuf_base
        w = sb("w", [P, 2, KC, H], f32)
        m_fourth = nc.alloc_sbuf_tensor_at("m_fourth", [P, N], f32r, offset=weights_at)
        onehot_r = sb("onehot_r", [P, T, P], f32r)
        oh = sb("oh", [EP, 2, OC, P], bf16)
        xsub = sb("xsub", [P, H], f32)
        xobj = sb("xobj", [P, H], f32)
        xsub_t = sb("xsub_t", [P, KC, P], f32)
        xobj_t = sb("xobj_t", [P, KC, P], f32)
        q_sb = xsub_t[:, :, :].rearrange("p k n -> p (k n)")
        qk = xsub[:, :]
        cs = sb("cs", [P, T, P], bf16)
        ed_in = sb("ed_in", [EP, EC, 2], i32)
        split = xsub[0:EP, 0:4 * EC].bitcast(i32)
        vals = sb("vals", [EP, EC, 5], bf16)
        idx = sb("idx", [EP, EC], i32)
        distinct = sb("distinct", [EP, EC], f32)
        adjv = sb("adjv", [EP, EC], f32)
        live = sb("live", [EP, EC], f32)
        incl = adjv
        rank = distinct
        tot = sb("tot", [EP, LOTS], bf16)
        base = sb("base", [EP, LOTS], f32)
        live_total = sb("live_total", [1, 1], i32)
        ones_f = sb("ones_f", [P, P], f32)
        ones_b = sb("ones_b", [P, P], bf16)
        ones_r = sb("ones_r", [P, 2], f32r)
        ident = sb("ident", [P, P], f32)
        before = sb("before", [P, P], bf16)
        earlier = sb("earlier", [P, P], bf16)
        slot_no = sb("slot_no", [P, P], f32)
        col_no = sb("col_no", [P, P], f32)
        row_no = sb("row_no", [P, T], f32)
        tile_no = sb("tile_no", [P, T], f32)
        brow = oh[0:1, :, :, :].rearrange("p a n s -> p (a n s)").bitcast(f32)[:, 0:2 * H].rearrange("p (a n) -> p a n", a=2)
        diag = sb("diag", [P, T], f32)
        slot = sb("slot", [P, 5], f32)
        ids = sb("ids", [P, 2], f32)
        ids_i = sb("ids_i", [P, 2], i32)
        subm = sb("subm", [P, 1], f32)
        key = sb("key", [P, 1], f32)
        subt = sb("subt", [P, T], f32)
        nvalid = sb("nvalid", [P, 1], f32)
        att = sb("att", [P, HEADS], f32)
        mx = sb("mx", [P, HEADS], f32)
        flags = sb("flags", [P, 2], f32)
        keep = sb("keep", [P, 2], f32)
        cen = sb("cen", [P, HEADS], f32)
        pexp = sb("pexp", [P, HEADS], f32)
        rv = sb("rv", [P, 2 * HEADS + 1], f32)
        ct = sb("ct", [P, HEADS], f32)
        c0 = sb("c0", [P, 1], f32)
        cf = sb("cf", [P, 1], f32)
        cnt = sb("cnt", [P, T], f32)
        wrow = sb("wrow", [P, T], f32)
        drow = sb("drow", [P, T], f32)
        eps = sb("eps", [P, 1], f32)
        dsc = sb("dsc", [P, 1], f32)
        w_flat = w[:, :, :, :].rearrange("p a k n -> p (a k n)")
        masked = w_flat[:, 0:HEADS * P].rearrange("p (h e) -> p h e", h=HEADS)
        rm = [w_flat[:, T * HEADS * i:T * HEADS * (i + 1)].rearrange("p (t h) -> p t h", t=T) for i in range(4)]
        onehot_t = w_flat[:, 2048:4096].rearrange("p (t e) -> p t e", t=T)
        pack = a[:, 0, 0:T * (HEADS + 1)].rearrange("p (t h) -> p t h", t=T)
        stats = a[:, 0, 256:256 + 6 * T].rearrange("p (t c) -> p t c", t=T)
        mv = a[:, 0, 384:384 + 2 * T].rearrange("p (t c) -> p t c", t=T)
        pen = a[:, 0, 640:768]
        same = a[:, 0, 768:1024].rearrange("p (a e) -> p a e", a=2)
        wd, sd, rs, sh = [a[:, 0, 512 + T * i:512 + T * (i + 1)] for i in range(4)]

        pool_f = nc.alloc_sbuf_tensor_at("slot_tiles", [P, 2 * T * H], f32, offset=high_at)
        taken = [0]

        def part(*dims):
            size = 1
            for n in dims:
                size *= n
            at = taken[0]
            taken[0] += size
            flat = pool_f[:, at:at + size]
            return flat if len(dims) == 1 else flat.rearrange("p (a b) -> p a b", a=dims[0])

        g_corr = part(T, H)
        g_sub, g_key, g_nvalid, g_valid = part(NT), part(NT), part(NT), part(NT)
        g_ids, g_keep = part(NT, 2), part(NT, 2)
        g_att, g_max = part(NT, HEADS), part(NT, HEADS)
        g_bias = part(2, H)[0:1]
        g_slot_no = part(P)
        g_firsts = part(NT)
        g_first, g_offset = part(1), part(1)
        g_diff = part(P)
        g_earlier = part(P)
        c_sub, c_key, c_max, c_flags = part(1), part(1), part(HEADS), part(2)
        g_table = part(T, 2 * HEADS + 1)

        def at(t):
            return bass.ds(t, 1)

        def weighted(t):
            return prod[:, t, :] if t < SAVED else w[:, 0, t - SAVED, :]

        def mask_of(t):
            if t in (3, T - 1):
                return m_fourth[:, :] if t == 3 else m_last[:, :]
            return m[:, t if t < 3 else (t - 4) % 3, :]

        a_round = a[:, :, 0:2 * P * FIRST].rearrange("p b (t n) -> p b t n", t=FIRST)
        ROUND_MASKS = 2 * NR

        cx = xobj[:, :]
        cx_parts = nc.alloc_sbuf_tensor_at("cx_parts", [P, 2, H], f32r, offset=weights_at + 4 * 2048)
        cx_high, cx_low = cx_parts[:, 0, :], cx_parts[:, 1, :]

        main = pb("main", [P, 4, H])
        e0, e1, e2, e3 = [pb(f"e{i}", [P, H]) for i in range(4)]
        RT = 2 * HEADS + 1
        table = e0[:, 32:32 + T * RT].rearrange("p (t c) -> p t c", t=T)
        counts = e0[:, 304:304 + 2 * T].rearrange("p (t c) -> p t c", t=T)

        def corr_bank(t):
            return [e1, e3, e0, e2][t % 4]

        block = ctx.enter_context(nc.Block())

        @block.sync
        def _(sp):
            sp.dma_start(ed_in[:, :, :], edges.rearrange("(p c) t -> p c t", p=EP)).then_inc(sem.edges_in, 16)
            for r, (k0, n) in enumerate(zip(STARTS, ROUNDS)):
                if r >= 2:
                    sp.wait_ge(sem.masks_made, 2 * (r - 1))
                sp.dma_start(a_round[:, r % 2, :, 0:n * P],
                             adj_blocks[0:FIRST, :, k0 * P:(k0 + n) * P].rearrange("t p n -> p t n")).then_inc(a_first[r % 2], 16)
                sp.dma_start(xs[:, k0:k0 + n, :],
                             x[k0 * P:(k0 + n) * P, :].rearrange("(k p) c -> p k c", p=P)).then_inc(x_r[r], 16)
            for t in range(FIRST, T):
                sp.wait_ge(sem.masks_made, ROUND_MASKS - 2 * ((NR - 1 - t) % 2) if t < FIRST + 2 else ROUND_MASKS + t - 5)
                sp.dma_start(a[:, t % 2, :], adj_blocks[t]).then_inc(a_par[t % 2], 16)
                if t == FIRST + 3:
                    sp.wait_ge(sem.products, FIRST)
                    sp.wait_ge(sem.column_sums, FIRST)
                    sp.dma_start(w[:, 0, :, :], wq_t.rearrange("(k p) n -> p k n", p=P)).then_inc(sem.weights_in, 16)
                    sp.dma_start(w[:, 1, :, :], wk_t.rearrange("(k p) n -> p k n", p=P)).then_inc(sem.weights_in, 16)
            sp.wait_ge(one.slots, 1)
            sp.dma_start(brow[:, 0, :], bq.rearrange("(a n) -> a n", a=1)).then_inc(sem.bq_in, 16)
            sp.dma_start(brow[:, 1, :], bk.rearrange("(a n) -> a n", a=1)).then_inc(sem.bk_in, 16)
            for t in range(T):
                sp.wait_ge(sem.y_done, t + 1)
                sp.dma_start(out[t * P:(t + 1) * P, :], xs[:, t, :]).then_inc(sem.out_done, 16)
            sp.wait_ge(sem.out_done, 16 * T)

        def general_branch(eng):
            eng.wait_ge(sem.live_count, 1)
            return eng.value_load(live_total[0:1, 0:1], min_val=0, max_val=E) > P

        @block.gpsimd
        def _(gp):
            g = nc.gpsimd
            g.memset(before[:, :], 1.0).then_inc(sem.const_pool, 1)
            g.memset(earlier[:, :], 1.0).then_inc(sem.const_pool, 1)
            g.memset(ident[:, :], 0.0).then_inc(sem.const_pool, 1)
            gp.wait_ge(sem.const_pool, 3)
            g.affine_select(out=before[:, :], in_=before[:, :], compare_op=ALU.is_gt, fill=0.0,
                            base=0, pattern=[[1, P]], channel_multiplier=-1).then_inc(sem.const_eye, 1)
            g.affine_select(out=earlier[:, :], in_=earlier[:, :], compare_op=ALU.is_gt, fill=0.0,
                            base=0, pattern=[[-1, P]], channel_multiplier=1).then_inc(sem.const_eye, 1)
            g.affine_select(out=ident[:, :], in_=ident[:, :], compare_op=ALU.not_equal, fill=1.0,
                            base=0, pattern=[[-1, P]], channel_multiplier=1).then_inc(sem.const_eye, 1)
            g.iota(slot_no[:, :], [[1, P]], 1, 0, allow_small_or_imprecise_dtypes=True).then_inc(sem.const_eye, 1)
            g.iota(col_no[:, :], [[1, P]], 0, 0, allow_small_or_imprecise_dtypes=True).then_inc(sem.const_eye, 1)
            g.iota(row_no[:, :], [[P, T]], 0, 1, allow_small_or_imprecise_dtypes=True).then_inc(sem.const_eye, 1)
            g.iota(tile_no[:, :], [[P, T]], 0, 0, allow_small_or_imprecise_dtypes=True).then_inc(sem.const_eye, 1)
            gp.wait_ge(sem.edge_index, 1)
            flat = adj.rearrange("i (j o) -> (i j) o", o=1)
            for c in range(EC):
                g.indirect_dma_start(adjv[:, c:c + 1], None, flat,
                                     bass.IndirectOffsetOnAxis(idx[:, c:c + 1].bitcast(u32), 0)).then_inc(adj_lot[c // LC], 16)

            def gather_x(s, r, end, done):
                gp.wait_ge(s, r + 1)
                gp.nop(nofuse=True)
                g.indirect_dma_start([xsub, xobj][end][:, :], None, x,
                                     bass.IndirectOffsetOnAxis(ids_i[:, end:end + 1].bitcast(u32), 0)).then_inc(done, 16)

            gather_x(one.slot_index, 0, 0, one.x_sub)
            gather_x(one.slot_index, 0, 1, one.x_obj)
            with gp.If(general_branch(gp)):
                with gp.Fori(0, NT) as t:
                    gather_x(one.slot_index, t + 1, 0, one.x_sub)
                    gather_x(one.slot_index, t + 1, 1, one.x_obj)
                with gp.Fori(0, NT) as t:
                    gather_x(gout.loaded, 6 * t + 5, 1, gout.x_obj)
            gp.wait_ge(sem.d_coef, 1)
            for t in range(T):
                if t % 2 == 0:
                    g.tensor_scalar(xs[:, t, :], xs[:, t, :], drow[:, t:t + 1], 1.0, ALU.mult, ALU.mult).then_inc(sem.x_scaled, 1)
                    gp.wait_ge(sem.x_scaled, t // 2 + 1)
                else:
                    gp.wait_ge(sem.x_scaled_act, (t + 1) // 2)
                gp.wait_ge(sem.weighted, t + 1)
                g.tensor_tensor(xs[:, t, :], xs[:, t, :], weighted(t), ALU.add).then_inc(sem.base, 1)

        @block.scalar
        def _(act):
            copy = nc.scalar.activation
            act.dma_start(diag[:, :], adj_diag).then_inc(sem.diag_in, 16)
            for r, (k0, n) in enumerate(zip(STARTS, ROUNDS)):
                act.wait_ge(x_r[r], 16)
                copy(xh[:, k0:k0 + n, :], xs[:, k0:k0 + n, :], ACT.Copy).then_inc(sem.x_high, 1)
            for t in range(SAVED):
                act.wait_ge(sem.products, t + 1)
                copy(prod[:, t, :], main[:, t % 4, :], ACT.Copy).then_inc(sem.product_saved, 1)

            def turned_and_q(s, r):
                act.wait_ge(s.sub_turned, r + 1)
                copy(xsub_t[:, :, :], e1[:, :].rearrange("p (k n) -> p k n", k=KC), ACT.Copy).then_inc(s.sub_turned_sbuf, 1)
                act.wait_ge(s.obj_turned, r + 1)
                copy(xobj_t[:, :, :], e0[:, :].rearrange("p (k n) -> p k n", k=KC), ACT.Copy).then_inc(s.obj_turned_sbuf, 1)
                act.wait_ge(s.q_done, r + 1)
                copy(q_sb, e3[:, :], ACT.Copy).then_inc(s.q_sbuf, 1)

            def edge_exp(s, r):
                act.wait_ge(s.centred, r + 1)
                copy(pexp[:, :], cen[:, :], ACT.Exp).then_inc(s.exps, 1)

            def high_part(s, r):
                act.wait_ge(s.cx, r + 1)
                copy(cx_high, cx, ACT.Copy).then_inc(s.cx_high, 1)

            def row_exps():
                act.wait_ge(sem.row_max, 1)
                copy(rm[1], rm[0], ACT.Exp, scale=-1.0).then_inc(sem.row_e0, 1)
                copy(rm[2], rm[0], ACT.Exp, scale=-1.0, bias=dsc[:, 0:1]).then_inc(sem.row_ed, 1)

            def scale_and_normalise():
                act.wait_ge(sem.d_coef, 1)

                def scale(t):
                    if t >= SAVED:
                        act.wait_ge(sem.products, t + 1)
                    src = prod[:, t, :] if t < SAVED else main[:, t % 4, :]
                    copy(weighted(t), src, ACT.Copy, scale=wrow[:, t:t + 1]).then_inc(sem.weighted, 1)
                    if t % 2:
                        copy(xs[:, t, :], xs[:, t, :], ACT.Copy, scale=drow[:, t:t + 1]).then_inc(sem.x_scaled_act, 1)

                def normalise(g):
                    t0, t1 = GROUPS[g]
                    act.wait_ge(sem.aggr, t1)
                    copy(sd[:, t0:t1], mv[:, t0:t1, 1], ACT.Sqrt, bias=eps[:, 0:1]).then_inc(sem.std, 1)
                    act.wait_ge(sem.shift, g + 1)
                    for t in range(t0, t1):
                        copy(xs[:, t, :], xs[:, t, :], ACT.Identity, scale=rs[:, t:t + 1],
                             bias=sh[:, t:t + 1]).then_inc(sem.y_done, 1)

                for t in range(4):
                    scale(t)
                high_part(one, 0)
                for t in range(4, 14):
                    scale(t)
                normalise(0)
                scale(14)
                normalise(1)
                scale(15)
                for g in range(2, len(GROUPS)):
                    normalise(g)

            turned_and_q(one, 0)
            with act.If(general_branch(act)):
                with act.Fori(0, NT) as t:
                    turned_and_q(one, t + 1)
                with act.Fori(0, NT) as t:
                    edge_exp(one, t)
                row_exps()
                with act.Fori(0, NT - 1) as t:
                    edge_exp(one, NT + t)
                    high_part(gout, t)
                edge_exp(one, 2 * NT - 1)
                scale_and_normalise()
            with act.Else():
                edge_exp(one, 0)
                row_exps()
                scale_and_normalise()

        @block.vector
        def _(dve):
            v = nc.vector
            dve.wait_ge(sem.edges_in, 16)
            v.scalar_tensor_tensor(idx[:, :], ed_in[:, :, 0], float(N), ed_in[:, :, 1], ALU.mult, ALU.add).then_inc(sem.edge_index, 1)
            flat = ed_in[:, :, :].rearrange("p c t -> p (c t)")
            v.tensor_scalar(split[:, 0:2 * EC], flat, 4, None, ALU.logical_shift_right).then_inc(sem.edge_split, 1)
            v.tensor_scalar(split[:, 2 * EC:4 * EC], flat, 15, None, ALU.bitwise_and).then_inc(sem.edge_split, 1)
            dve.wait_ge(sem.edge_split, 2)
            v.tensor_copy(vals[:, :, 0:2], split[:, 0:2 * EC].rearrange("p (c t) -> p c t", t=2)).then_inc(sem.edge_values, 1)
            v.tensor_copy(vals[:, :, 2:4], split[:, 2 * EC:4 * EC].rearrange("p (c t) -> p c t", t=2)).then_inc(sem.edge_values, 1)
            v.memset(vals[:, :, 4:5], 1.0).then_inc(sem.edge_values, 1)
            v.tensor_tensor(distinct[:, :], ed_in[:, :, 0], ed_in[:, :, 1], ALU.not_equal).then_inc(sem.edge_distinct, 1)
            v.memset(ones_f[:, :], 1.0).then_inc(sem.const_vector, 1)
            v.memset(ones_b[:, :], 1.0).then_inc(sem.const_vector, 1)
            dve.wait_ge(sem.const_vector, 1)
            v.tensor_copy(ones_r[:, :], ones_f[:, 0:2]).then_inc(sem.const_vector, 1)
            v.memset(eps[:, :], EPS).then_inc(sem.const_vector, 1)
            v.memset(dsc[:, :], DIAG_SCORE).then_inc(sem.const_vector, 1)
            for r, (k0, n) in enumerate(zip(STARTS, ROUNDS)):
                cols = slice(k0 * P, (k0 + n) * P)
                dve.wait_ge(a_first[r % 2], 16 * (r // 2 + 1))
                v.tensor_scalar(m[:, :, cols], a_round[:, r % 2, 0:3, 0:n * P], 1.0, None, ALU.is_equal).then_inc(sem.masks_made, 1)
                v.tensor_scalar(m_fourth[:, cols], a_round[:, r % 2, 3, 0:n * P], 1.0, None, ALU.is_equal).then_inc(sem.masks_made, 1)
                dve.wait_ge(sem.x_high, r + 1)
                v.tensor_tensor(xl[:, k0:k0 + n, :], xs[:, k0:k0 + n, :], xh[:, k0:k0 + n, :].bitcast(f32),
                                ALU.subtract).then_inc(sem.x_low, 1)

            def mask(t):
                dve.wait_ge(a_par[t % 2], 16 * (t // 2 - 1))
                if t < T - 1:
                    u = t - 4 if t < 7 else t - 3
                    dve.wait_ge(sem.products, u + 1)
                    dve.wait_ge(sem.column_sums, u + 1)
                v.tensor_scalar(mask_of(t), a[:, t % 2, :], 1.0, None, ALU.is_equal).then_inc(sem.masks_made, 1)

            def column_sum(t):
                dve.wait_ge(sem.masks_made, ROUND_MASKS if t < FIRST else ROUND_MASKS + t - 3)
                with nc.allow_low_precision(reason="counts up to 16 are exact in bfloat16"):
                    v.tensor_reduce(cs[:, t, :], mask_of(t).bitcast(f32).rearrange("p (j i) -> p i j", j=T),
                                    AX.X, ALU.add).then_inc(sem.column_sums, 1)

            def lot_scan(n):
                cols = slice(n * LC, (n + 1) * LC)
                dve.wait_ge(adj_lot[n], 16 * LC)
                v.scalar_tensor_tensor(live[:, cols], adjv[:, cols], 1.0, distinct[:, cols], ALU.is_equal, ALU.mult).then_inc(sem.live, 1)
                dve.wait_ge(sem.live, n + 1)
                v.tensor_tensor_scan(incl[:, cols], ones_f[0:EP, 0:LC], live[:, cols], 0.0, ALU.mult, ALU.add).then_inc(sem.scan, 1)
                dve.wait_ge(sem.scan, n + 1)
                v.tensor_copy(tot[:, n:n + 1], incl[:, (n + 1) * LC - 1:(n + 1) * LC]).then_inc(sem.totals, 1)

            def lot_ranks(n):
                cols = slice(n * LC, (n + 1) * LC)
                dve.wait_ge(sem.prefix, n + 1)
                v.tensor_copy(base[:, n:n + 1], e1[0:EP, 0:1]).then_inc(sem.prefix_copied, 1)
                if n == LOTS - 1:
                    v.tensor_copy(live_total[:, :], e1[0:1, 1:2]).then_inc(sem.live_count, 1)
                dve.wait_ge(sem.prefix_copied, n + 1)
                v.scalar_tensor_tensor(rank[:, cols], incl[:, cols], base[:, n:n + 1], live[:, cols], ALU.add, ALU.mult).then_inc(sem.ranks, 1)
                dve.wait_ge(sem.ranks, n + 1)
                slot_onehots(one, 0, slot_no, range(n * LC // OC, (n + 1) * LC // OC))

            def slot_onehots(s, r, numbers, lots=range(NOC)):
                for c in lots:
                    if c >= 2:
                        dve.wait_ge(s.onehot_used, (NOC - 1) * r + c - 1)
                    v.tensor_tensor(oh[:, c % 2, :, :],
                                    numbers[0:EP, :].unsqueeze(1).broadcast_to([EP, OC, P]),
                                    rank[:, c * OC:(c + 1) * OC].unsqueeze(2).broadcast_to([EP, OC, P]),
                                    ALU.is_equal).then_inc(s.onehot_made, 1)

            def slot_ids(s, r):
                dve.wait_ge(s.slots, r + 1)
                v.tensor_copy(slot[:, :], e0[:, 0:5]).then_inc(s.slots_copied, 1)
                dve.wait_ge(s.slots_copied, r + 1)
                v.scalar_tensor_tensor(ids[:, :], slot[:, 0:2], 16.0, slot[:, 2:4], ALU.mult, ALU.add).then_inc(s.slot_ids, 1)
                dve.wait_ge(s.slot_ids, r + 1)
                v.tensor_copy(ids_i[:, :], ids[:, :]).then_inc(s.slot_index, 1)
                v.scalar_tensor_tensor(subm[:, :], ids[:, 0:1], -1.0, slot[:, 4:5], ALU.add, ALU.add).then_inc(s.slot_sub, 1)
                v.scalar_tensor_tensor(key[:, :], ids[:, 0:1], float(N), ids[:, 1:2], ALU.mult, ALU.add).then_inc(s.slot_key, 1)
                v.tensor_scalar(nvalid[:, :], slot[:, 4:5], -1.0, None, ALU.mult).then_inc(s.slot_key, 1)

            def row_onehot(s, r):
                v.tensor_scalar(subt[:, :], tile_no[:, :], subm[:, 0:1], -1.0, ALU.subtract, ALU.mult).then_inc(s.sub_tiles, 1)
                dve.wait_ge(s.sub_tiles, r + 1)
                v.tensor_tensor(onehot_r[:, :, :], col_no[:, :].unsqueeze(1).broadcast_to([P, T, P]),
                                subt[:, :].unsqueeze(2).broadcast_to([P, T, P]), ALU.is_equal).then_inc(s.row_onehot, 1)

            def row_onehot_t(s, r, rows):
                dve.wait_ge(rows, r + 1)
                v.tensor_tensor(onehot_t, e2[:, 0:P].unsqueeze(1).broadcast_to([P, T, P]),
                                row_no[:, :].unsqueeze(2).broadcast_to([P, T, P]), ALU.is_equal).then_inc(s.row_onehot_t, 1)

            def edge_scores(s, r, k_bank):
                dve.wait_ge(s.q_sbuf, r + 1)
                dve.wait_ge(s.k_done, r + 1)
                v.tensor_tensor(qk, k_bank, q_sb, ALU.mult).then_inc(s.qk_product, 1)
                dve.wait_ge(s.qk_product, r + 1)
                v.tensor_reduce(att[:, :], qk.rearrange("p (h d) -> p h d", h=HEADS), AX.X, ALU.add).then_inc(s.qk_sum, 1)
                dve.wait_ge(s.qk_sum, r + 1)
                v.tensor_scalar(att[:, :], att[:, :], float(DK) ** -0.5, None, ALU.mult).then_inc(s.att, 1)

            def pair_flags(s, r, col_sub, col_key, mask):
                dve.wait_ge(s.id_rows, r + 1)
                v.tensor_scalar(pen, e2[:, 0:P], col_sub, -BIG, ALU.not_equal, ALU.mult).then_inc(s.other_row, 1)
                v.scalar_tensor_tensor(same[:, 0, :], e2[:, 0:P], col_sub, mask, ALU.is_equal, ALU.mult).then_inc(s.id_flags, 1)
                v.scalar_tensor_tensor(same[:, 1, :], e2[:, P:2 * P], col_key, mask, ALU.is_equal, ALU.mult).then_inc(s.id_flags, 1)
                dve.wait_ge(s.id_flags, 2 * r + 2)
                v.tensor_reduce(flags[:, :], same, AX.X, ALU.max).then_inc(s.flag_max, 1)

            def pair_max(s, r):
                penb = pen.unsqueeze(1).broadcast_to([P, 4, P])
                dve.wait_ge(s.other_row, r + 1)
                dve.wait_ge(s.att_rows_a, r + 1)
                v.tensor_tensor(masked[:, 0:4, :], e1[:, :].rearrange("p (h e) -> p h e", h=4), penb, ALU.add).then_inc(s.masked_a, 1)
                dve.wait_ge(s.att_rows_b, r + 1)
                v.tensor_tensor(masked[:, 4:8, :], e3[:, :].rearrange("p (h e) -> p h e", h=4), penb, ALU.add).then_inc(s.masked_b, 1)
                dve.wait_ge(s.masked_a, r + 1)
                dve.wait_ge(s.masked_b, r + 1)
                v.tensor_reduce(mx[:, :], masked, AX.X, ALU.max).then_inc(s.score_max, 1)

            def centre(s):
                v.tensor_tensor(cen[:, :], att[:, :], mx[:, :], ALU.subtract).then_inc(s.centred, 1)

            def row_values(s, r):
                v.tensor_scalar(rv[:, 0:HEADS], mx[:, :], keep[:, 0:1], None, ALU.mult).then_inc(s.rowvals, 1)
                v.tensor_copy(rv[:, 2 * HEADS:RT], keep[:, 1:2]).then_inc(s.rowvals, 1)
                dve.wait_ge(s.exps, r + 1)
                v.tensor_scalar(rv[:, HEADS:2 * HEADS], pexp[:, :], keep[:, 1:2], None, ALU.mult).then_inc(s.rowvals, 1)

            def coefficients(s, r):
                dve.wait_ge(s.gathered, r + 1)
                v.tensor_tensor(ct[:, :], e2[:, 0:HEADS], pexp[:, :], ALU.mult).then_inc(s.coef_terms, 1)
                dve.wait_ge(s.coef_terms, r + 1)
                v.tensor_reduce(c0[:, :], ct[:, :], AX.X, ALU.add).then_inc(s.coef_sum, 1)
                dve.wait_ge(s.coef_sum, r + 1)
                v.scalar_tensor_tensor(cf[:, :], c0[:, :], 1.0 / HEADS, e2[:, HEADS:HEADS + 1], ALU.mult, ALU.subtract).then_inc(s.coef_diff, 1)
                dve.wait_ge(s.coef_diff, r + 1)
                v.tensor_tensor(cf[:, :], cf[:, :], keep[:, 1:2], ALU.mult).then_inc(s.coef, 1)
                dve.wait_ge(s.coef, r + 1)
                v.tensor_scalar(cx, cx, cf[:, 0:1], None, ALU.mult).then_inc(s.cx, 1)

            def low_part(s, r):
                dve.wait_ge(s.cx_high, r + 1)
                v.tensor_tensor(cx_low, cx, cx_high.bitcast(f32), ALU.subtract).then_inc(s.cx_low, 1)

            def load_tile(s, t):
                v.tensor_copy(subm[:, :], g_sub[:, at(t)]).then_inc(s.loaded, 1)
                v.tensor_copy(att[:, :].unsqueeze(1), g_att[:, at(t), :]).then_inc(s.loaded, 1)
                v.tensor_copy(mx[:, :].unsqueeze(1), g_max[:, at(t), :]).then_inc(s.loaded, 1)
                v.tensor_copy(keep[:, :].unsqueeze(1), g_keep[:, at(t), :]).then_inc(s.loaded, 1)
                v.tensor_copy(key[:, :], g_key[:, at(t)]).then_inc(s.loaded, 1)

            def softmax_rows():
                dve.wait_ge(sem.row_table, 1)
                v.tensor_scalar(rm[0], table[:, :, 0:HEADS], DIAG_SCORE, None, ALU.max).then_inc(sem.row_max, 1)
                dve.wait_ge(sem.counts_copied, 1)
                v.tensor_tensor(cnt[:, :], cnt[:, :], table[:, :, 2 * HEADS], ALU.subtract).then_inc(sem.counts_copied, 1)
                dve.wait_ge(sem.counts_copied, 2)
                v.tensor_tensor(cnt[:, :], cnt[:, :], diag[:, :], ALU.subtract).then_inc(sem.zero_count, 1)
                dve.wait_ge(sem.zero_count, 1)
                dve.wait_ge(sem.row_e0, 1)
                v.tensor_tensor(rm[3], rm[1], cnt[:, :].unsqueeze(2).broadcast_to([P, T, HEADS]), ALU.mult).then_inc(sem.den_a, 1)
                dve.wait_ge(sem.den_a, 1)
                v.tensor_tensor(rm[3], rm[3], table[:, :, HEADS:2 * HEADS], ALU.add).then_inc(sem.den_b, 1)
                dve.wait_ge(sem.den_b, 1)
                dve.wait_ge(sem.row_ed, 1)
                v.tensor_tensor(rm[3], rm[3], rm[2], ALU.add).then_inc(sem.den_c, 1)
                dve.wait_ge(sem.den_c, 1)
                v.reciprocal(pack[:, :, 0:HEADS], rm[3]).then_inc(sem.row_r, 1)
                dve.wait_ge(sem.row_r, 1)
                v.tensor_tensor(rm[1], rm[1], pack[:, :, 0:HEADS], ALU.mult).then_inc(sem.w_terms, 1)
                v.tensor_tensor(rm[2], rm[2], pack[:, :, 0:HEADS], ALU.mult).then_inc(sem.d_terms, 1)
                dve.wait_ge(sem.w_terms, 1)
                v.tensor_reduce(wrow[:, :], rm[1], AX.X, ALU.add).then_inc(sem.w_sum, 1)
                dve.wait_ge(sem.d_terms, 1)
                v.tensor_reduce(drow[:, :], rm[2], AX.X, ALU.add).then_inc(sem.d_sum, 1)
                dve.wait_ge(sem.w_sum, 1)
                v.tensor_scalar(wrow[:, :], wrow[:, :], 1.0 / HEADS, None, ALU.mult).then_inc(sem.w_done, 1)
                dve.wait_ge(sem.w_done, 1)
                v.tensor_copy(pack[:, :, HEADS], wrow[:, :]).then_inc(sem.row_pack, 1)
                v.tensor_tensor(wd[:, :], wrow[:, :], diag[:, :], ALU.mult).then_inc(sem.w_diag, 1)
                dve.wait_ge(sem.d_sum, 1)
                dve.wait_ge(sem.w_diag, 1)
                v.scalar_tensor_tensor(drow[:, :], drow[:, :], 1.0 / HEADS, wd[:, :], ALU.mult, ALU.subtract).then_inc(sem.w_diag, 1)
                dve.wait_ge(sem.w_diag, 2)
                v.tensor_scalar(drow[:, :], drow[:, :], 1.0, None, ALU.add).then_inc(sem.d_coef, 1)

            def output_rows():
                low_part(one, 0)
                for t in range(T):
                    dve.wait_ge(sem.corr, t + 1)
                    dve.wait_ge(sem.base, t + 1)
                    v.tensor_tensor(xs[:, t, :], xs[:, t, :], corr_bank(t)[:, :], ALU.add).then_inc(sem.y_sum, 1)
                    dve.wait_ge(sem.y_sum, t + 1)
                    v.bn_stats(stats[:, t, :], xs[:, t, :]).then_inc(sem.stats, 1)
                    dve.wait_ge(sem.stats, t + 1)
                    v.bn_aggr(mv[:, t, :], stats[:, t, :]).then_inc(sem.aggr, 1)
                    for g, (t0, t1) in enumerate(GROUPS):
                        if t1 != (t if t < T - 1 else T) and not (t == T - 1 and t1 == T - 1):
                            continue
                        sl = slice(t0, t1)
                        dve.wait_ge(sem.std, g + 1)
                        v.reciprocal(rs[:, sl], sd[:, sl]).then_inc(sem.rstd, 1)
                        dve.wait_ge(sem.rstd, g + 1)
                        v.scalar_tensor_tensor(sh[:, sl], mv[:, sl, 0], -1.0, rs[:, sl], ALU.mult, ALU.mult).then_inc(sem.shift, 1)

            dve.wait_ge(sem.diag_in, 16)
            v.tensor_scalar(diag[:, :], diag[:, :], 1.0, None, ALU.is_equal).then_inc(sem.diag_flag, 1)
            dve.wait_ge(sem.diag_flag, 1)
            dve.wait_ge(sem.edge_distinct, 1)
            dve.wait_ge(sem.const_vector, 5)
            dve.wait_ge(sem.const_eye, 7)
            lot_scan(0)
            for t in range(FIRST):
                column_sum(t)
                if t < 3:
                    mask(t + 4)
                if t == 1:
                    lot_ranks(0)
            for t in range(7, 14):
                column_sum(t - 3)
                mask(t)
                if t in (8, 10, 13):
                    lot_scan((t - 5) // 2 - (t == 13))
                if t in (9, 11):
                    lot_ranks((t - 7) // 2)
            lot_ranks(3)
            column_sum(11)
            slot_ids(one, 0)
            mask(14)
            dve.wait_ge(one.slot_sub, 1)
            row_onehot(one, 0)
            column_sum(12)
            mask(15)
            with dve.If(general_branch(dve)):
                column_sum(13)
                edge_scores(one, 0, main[:, 3, :])
                dve.wait_ge(sem.counts, 1)
                v.tensor_copy(cnt[:, :].unsqueeze(2), counts[:, :, 0:1]).then_inc(sem.counts_copied, 1)
                dve.wait_ge(sem.products, T)
                dve.wait_ge(sem.bq_in, 16)
                dve.wait_ge(sem.bk_in, 16)
                dve.wait_ge(one.att, 1)
                v.tensor_copy(g_bias, brow).then_inc(gen.prepared, 1)
                v.memset(g_first, -float(P)).then_inc(gen.stored, 1)
                v.tensor_scalar(g_diff, col_no[:, :], row_no[:, 0:1], None, ALU.subtract).then_inc(gen.prepared, 1)
                dve.wait_ge(gen.prepared, 2)
                with dve.Fori(0, NT) as t:
                    dve.wait_ge(gen.stored, 7 * t + 1)
                    v.tensor_scalar(g_first, g_first, float(P), None, ALU.add).then_inc(gen.first_slot, 1)
                    dve.wait_ge(gen.first_slot, t + 1)
                    v.tensor_scalar(g_slot_no, slot_no[:, :], g_first, None, ALU.add).then_inc(gen.slot_shift, 1)
                    dve.wait_ge(gen.slot_shift, t + 1)
                    slot_onehots(one, t + 1, g_slot_no)
                    slot_ids(one, t + 1)
                    edge_scores(one, t + 1, e1[:, :])
                    dve.wait_ge(one.att, t + 2)
                    v.tensor_copy(g_att[:, at(t), :], att[:, :].unsqueeze(1)).then_inc(gen.stored, 1)
                    v.tensor_copy(g_sub[:, at(t)], subm[:, :]).then_inc(gen.stored, 1)
                    v.tensor_copy(g_key[:, at(t)], key[:, :]).then_inc(gen.stored, 1)
                    v.tensor_copy(g_nvalid[:, at(t)], nvalid[:, :]).then_inc(gen.stored, 1)
                    v.tensor_copy(g_valid[:, at(t)], slot[:, 4:5]).then_inc(gen.stored, 1)
                    v.tensor_copy(g_ids[:, at(t), :], ids[:, :].unsqueeze(1)).then_inc(gen.stored, 1)
                    v.tensor_copy(g_firsts[:, at(t)], g_first).then_inc(gen.stored, 1)
                v.memset(g_offset, 0.0).then_inc(gpair.score_join, 1)
                v.memset(c_flags, 0.0).then_inc(gpair.kept, 1)
                with dve.Fori(0, NT) as c:
                    dve.wait_ge(gen.stored, 7 * NT + 1)
                    dve.wait_ge(gpair.kept, 2 * c + 1)
                    v.tensor_copy(c_sub, g_sub[:, at(c)]).then_inc(gpair.column_loaded, 1)
                    v.tensor_copy(c_key, g_key[:, at(c)]).then_inc(gpair.column_loaded, 1)
                    v.memset(c_max, DIAG_SCORE).then_inc(gpair.column_loaded, 1)
                    v.memset(c_flags, 0.0).then_inc(gpair.column_loaded, 1)
                    with dve.Fori(0, NT) as r:
                        n = c * NT + r
                        dve.wait_ge(gpair.column_loaded, 4 * c + 4)
                        dve.wait_ge(gpair.score_join, n + 1)
                        v.tensor_copy(subm[:, :], g_sub[:, at(r)]).then_inc(gpair.row_loaded, 1)
                        v.tensor_copy(key[:, :], g_key[:, at(r)]).then_inc(gpair.row_loaded, 1)
                        v.tensor_copy(att[:, :].unsqueeze(1), g_att[:, at(r), :]).then_inc(gpair.row_loaded, 1)
                        v.tensor_tensor(g_offset, g_firsts[:, at(c)], g_firsts[:, at(r)], ALU.subtract).then_inc(gpair.offset, 1)
                        dve.wait_ge(gpair.offset, n + 1)
                        v.tensor_scalar(g_earlier, g_diff, g_offset, None, ALU.is_lt).then_inc(gpair.mask, 1)
                        dve.wait_ge(gpair.mask, n + 1)
                        pair_flags(one, n, c_sub, c_key, g_earlier)
                        dve.wait_ge(one.flag_max, n + 1)
                        v.tensor_tensor(c_flags, c_flags, flags[:, :], ALU.max).then_inc(gpair.flag_join, 1)
                        pair_max(one, n)
                        dve.wait_ge(one.score_max, n + 1)
                        v.tensor_tensor(c_max, c_max, mx[:, :], ALU.max).then_inc(gpair.score_join, 1)
                    dve.wait_ge(gpair.flag_join, NT * c + NT)
                    dve.wait_ge(gpair.score_join, NT * c + NT + 1)
                    v.tensor_copy(nvalid[:, :], g_nvalid[:, at(c)]).then_inc(gpair.valid_loaded, 1)
                    v.tensor_copy(slot[:, 4:5], g_valid[:, at(c)]).then_inc(gpair.valid_loaded, 1)
                    v.tensor_copy(g_max[:, at(c), :], c_max.unsqueeze(1)).then_inc(gpair.kept, 1)
                    dve.wait_ge(gpair.valid_loaded, 2 * c + 2)
                    v.tensor_scalar(g_keep[:, at(c), :], c_flags.unsqueeze(1), nvalid[:, 0:1], slot[:, 4:5],
                                    ALU.mult, ALU.add).then_inc(gpair.kept, 1)
                v.memset(g_table, 0.0).then_inc(gval.table_added, 1)
                with dve.Fori(0, NT) as t:
                    dve.wait_ge(gpair.kept, 2 * NT + 1)
                    dve.wait_ge(gval.table_added, t + 1)
                    load_tile(gval, t)
                    dve.wait_ge(gval.loaded, 5 * t + 5)
                    centre(one)
                    row_onehot(one, t + 1)
                    row_values(one, t)
                    dve.wait_ge(one.table, t + 1)
                    v.tensor_tensor(g_table, g_table, table, ALU.add).then_inc(gval.table_added, 1)
                softmax_rows()
                v.memset(g_corr, 0.0).then_inc(gout.corr_added, 1)

                def tile_state(t):
                    load_tile(gout, t)
                    v.tensor_copy(ids_i[:, :].unsqueeze(1), g_ids[:, at(t), :]).then_inc(gout.loaded, 1)
                    dve.wait_ge(gout.loaded, 6 * t + 6)
                    centre(one)
                    row_onehot(one, NT + 1 + t)
                    row_onehot_t(gout, t, gout.id_rows)

                with dve.Fori(0, NT - 1) as t:
                    dve.wait_ge(gout.corr_added, T * t + 1)
                    tile_state(t)
                    dve.wait_ge(one.exps, NT + t + 1)
                    dve.wait_ge(gout.x_obj, 16 * t + 16)
                    coefficients(gout, t)
                    low_part(gout, t)
                    for i in range(T):
                        dve.wait_ge(gout.corr, T * t + i + 1)
                        v.tensor_tensor(g_corr[:, i, :], g_corr[:, i, :], corr_bank(i)[:, :], ALU.add).then_inc(gout.corr_added, 1)
                dve.wait_ge(gout.corr_added, T * (NT - 1) + 1)
                tile_state(NT - 1)
                dve.wait_ge(one.exps, 2 * NT)
                dve.wait_ge(gout.x_obj, 16 * NT)
                coefficients(one, 0)
                output_rows()
            with dve.Else():
                dve.wait_ge(one.slot_key, 2)
                dve.wait_ge(sem.masks_made, ROUND_MASKS + T - 5)
                pair_flags(one, 0, subm[:, 0:1], key[:, 0:1], earlier[:, :])
                dve.wait_ge(one.flag_max, 1)
                v.tensor_scalar(keep[:, :], flags[:, :], nvalid[:, 0:1], slot[:, 4:5], ALU.mult, ALU.add).then_inc(one.keep, 1)
                column_sum(13)
                edge_scores(one, 0, main[:, 3, :])
                pair_max(one, 0)
                dve.wait_ge(one.score_max, 1)
                v.tensor_scalar(mx[:, :], mx[:, :], DIAG_SCORE, None, ALU.max).then_inc(one.edge_max, 1)
                dve.wait_ge(one.edge_max, 1)
                dve.wait_ge(one.att, 1)
                centre(one)
                dve.wait_ge(one.keep, 1)
                row_values(one, 0)
                row_onehot_t(one, 0, one.id_rows)
                dve.wait_ge(sem.counts, 1)
                dve.wait_ge(sem.row_table, 1)
                v.tensor_copy(cnt[:, :].unsqueeze(2), counts[:, :, 0:1]).then_inc(sem.counts_copied, 1)
                softmax_rows()
                coefficients(one, 0)
                output_rows()

        @block.tensor
        def _(pe):
            mm = nc.tensor.matmul

            def product(t, k):
                mask = mask_of(t)[:, k * P:(k + 1) * P]
                mm(main[:, t % 4, :], mask, xh[:, k, :], start=(k == 0), stop=False)
                last = mm(main[:, t % 4, :], mask, xl[:, k, :], start=False, stop=(k == T - 1))
                if k == T - 1:
                    last.then_inc(sem.products, 1)

            def prefix(n):
                pe.wait_ge(sem.totals, n + 1)
                if n:
                    pe.wait_ge(sem.prefix_copied, n)
                else:
                    pe.wait_ge(sem.const_eye, 7)
                mm(e1[0:EP, 0:1], before[0:EP, 0:EP], tot[:, n:n + 1], start=True, stop=(n == 0))
                for i in range(n):
                    last = mm(e1[0:EP, 0:1], ones_b[0:EP, 0:EP], tot[:, i:i + 1], start=False, stop=(i == n - 1))
                for i in range(LOTS if n == LOTS - 1 else 1):
                    last = mm(e1[0:1, 1:2], ones_b[0:EP, 0:1], tot[:, i:i + 1], start=(i == 0), stop=(i == (LOTS - 1 if n == LOTS - 1 else 0)))
                last.then_inc(sem.prefix, 1)

            def compact(s, r, lots=range(NOC)):
                for c in lots:
                    pe.wait_ge(s.onehot_made, NOC * r + c + 1)
                    for n in range(OC):
                        last = mm(e0[:, 0:5], oh[:, c % 2, n, :], vals[:, c * OC + n, :],
                                  start=(c == 0 and n == 0), stop=(c == NOC - 1 and n == OC - 1))
                    last.then_inc(s.onehot_used if c < NOC - 1 else s.slots, 1)

            def compact_lot(n):
                compact(one, 0, range(n * LC // OC, (n + 1) * LC // OC))

            def turn(s, r):
                pe.wait_ge(s.x_sub, 16 * r + 16)
                for k in range(KC):
                    last = nc.tensor.transpose(e1[:, k * P:(k + 1) * P], xsub[:, k * P:(k + 1) * P], ident[:, :])
                last.then_inc(s.sub_turned, 1)
                pe.wait_ge(s.x_obj, 16 * r + 16)
                for k in range(KC):
                    last = nc.tensor.transpose(e0[:, k * P:(k + 1) * P], xobj[:, k * P:(k + 1) * P], ident[:, :])
                last.then_inc(s.obj_turned, 1)

            def bias_row(dst, bias):
                mm(dst, ones_f[0:1, :], bias, start=True, stop=False)

            def project(dst, src, weights, done):
                for k in range(KC):
                    last = mm(dst, src[:, k, :], weights[:, k, :], start=False, stop=(k == KC - 1))
                last.then_inc(done, 1)

            def along_free(dst, column):
                return mm(dst, column.broadcast_to([P, P]), ident[:, :], start=True, stop=True)

            def id_rows(s):
                along_free(e2[:, 0:P], subm[:, 0:1])
                along_free(e2[:, P:2 * P], key[:, 0:1]).then_inc(s.id_rows, 1)

            def att_rows(s):
                for dst, h0, done in ((e1, 0, s.att_rows_a), (e3, 4, s.att_rows_b)):
                    for h in range(4):
                        last = along_free(dst[:, h * P:(h + 1) * P], att[:, h0 + h:h0 + h + 1])
                    last.then_inc(done, 1)

            def row_counts():
                pe.wait_ge(one.obj_turned_sbuf, 1)
                pe.wait_ge(sem.column_sums, SUMMED)
                pe.wait_ge(sem.masks_made, ROUND_MASKS + T - 4)
                for t in range(SUMMED):
                    last = mm(counts[:, t, :], cs[:, t, :], ones_b[:, 0:2], start=True, stop=True)
                for t in range(SUMMED, T):
                    for k in range(T):
                        last = mm(counts[:, t, :], mask_of(t)[:, k * P:(k + 1) * P], ones_r[:, :],
                                  start=(k == 0), stop=(k == T - 1))
                last.then_inc(sem.counts, 1)

            def row_table(r, onehots, done):
                pe.wait_ge(one.rowvals, 3 * r + 3)
                pe.wait_ge(one.row_onehot, onehots)
                for t in range(T):
                    last = mm(table[:, t, :], onehot_r[:, t, :].bitcast(f32), rv[:, :], start=True, stop=True)
                last.then_inc(done, 1)

            def gather_back(s, r, done=None):
                pe.wait_ge(s.row_onehot_t, r + 1)
                for t in range(T):
                    last = mm(e2[:, 0:HEADS + 1], onehot_t[:, t, :], pack[:, t, :], start=(t == 0), stop=(t == T - 1))
                last.then_inc(done or s.gathered, 1)

            def corrections(s, r, done, used, first, general, tiles=range(T)):
                if tiles[0] == 0:
                    pe.wait_ge(s.cx_high, r + 1)
                    pe.wait_ge(s.cx_low, r + 1)
                for t in tiles:
                    if t >= 4:
                        pe.wait_ge(used, first + t - 3)
                    dst = corr_bank(t)
                    mm(dst[:, :], onehot_r[:, t, :], cx_high, start=True, stop=False)
                    last = mm(dst[:, :], onehot_r[:, t, :], cx_low, start=False, stop=not general)
                    if general:
                        last = mm(dst[:, :], ident[:, :], g_corr[:, t, :], start=False, stop=True)
                    last.then_inc(done, 1)

            def products(t, ks=range(T)):
                if ks[0] == 0:
                    pe.wait_ge(sem.masks_made, ROUND_MASKS + t - 3)
                    if t - 4 < SAVED:
                        pe.wait_ge(sem.product_saved, t - 3)
                for k in ks:
                    product(t, k)

            def biases():
                pe.wait_ge(sem.bq_in, 16)
                bias_row(e3[:, :], brow[:, 0, :])
                pe.wait_ge(sem.bk_in, 16)
                pe.wait_ge(sem.product_saved, SAVED)
                bias_row(main[:, 3, :], brow[:, 1, :])

            def queries_keys():
                pe.wait_ge(sem.weights_in, 32)
                pe.wait_ge(one.sub_turned_sbuf, 1)
                project(e3[:, :], xsub_t, w[:, 0, :, :], one.q_done)
                pe.wait_ge(one.obj_turned_sbuf, 1)
                project(main[:, 3, :], xobj_t, w[:, 1, :, :], one.k_done)

            def tiles_with(tiles, steps):
                for t in tiles:
                    at_k = [0] + sorted(k for tt, k in steps if tt == t and k) + [T]
                    for k0, k1 in zip(at_k, at_k[1:]):
                        for step in steps.get((t, k0), []):
                            step()
                        products(t, range(k0, k1))

            for r, (k0, n) in enumerate(zip(STARTS, ROUNDS)):
                pe.wait_ge(sem.masks_made, 2 * r + 2)
                pe.wait_ge(sem.x_low, r + 1)
                for t in range(FIRST):
                    for k in range(k0, k0 + n):
                        product(t, k)
            tiles_with(range(4, 12), {
                (4, 0): [lambda: prefix(0)], (5, 4): [lambda: compact_lot(0)],
                (7, 6): [lambda: prefix(1)], (8, 8): [lambda: compact_lot(1)],
                (9, 6): [lambda: prefix(2)], (10, 8): [lambda: compact_lot(2)],
                (11, 5): [lambda: prefix(3)], (11, 13): [lambda: compact_lot(3)],
            })
            with pe.If(general_branch(pe)):
                biases()
                turn(one, 0)
                queries_keys()
                pe.wait_ge(one.att, 1)
                tiles_with(range(12, 16), {})
                row_counts()
                pe.wait_ge(sem.counts_copied, 1)
                pe.wait_ge(gen.prepared, 2)
                with pe.Fori(0, NT) as t:
                    compact(one, t + 1)
                    turn(one, t + 1)
                    bias_row(e3[:, :], g_bias[:, 0, :])
                    pe.wait_ge(one.sub_turned_sbuf, t + 2)
                    project(e3[:, :], xsub_t, w[:, 0, :, :], one.q_done)
                    bias_row(e1[:, :], g_bias[:, 1, :])
                    pe.wait_ge(one.obj_turned_sbuf, t + 2)
                    project(e1[:, :], xobj_t, w[:, 1, :, :], one.k_done)
                with pe.Fori(0, NT) as c:
                    with pe.Fori(0, NT) as r:
                        n = c * NT + r
                        pe.wait_ge(gpair.row_loaded, 3 * n + 3)
                        id_rows(one)
                        att_rows(one)
                with pe.Fori(0, NT) as t:
                    row_table(t, t + 2, one.table)
                pe.wait_ge(gval.table_added, NT + 1)
                mm(e0[:, 32:32 + T * RT], ident[:, :], g_table.rearrange("p a b -> p (a b)"),
                   start=True, stop=True).then_inc(sem.row_table, 1)
                pe.wait_ge(sem.row_pack, 1)
                with pe.Fori(0, NT - 1) as t:
                    pe.wait_ge(gout.loaded, 6 * t + 6)
                    along_free(e2[:, 0:P], subm[:, 0:1]).then_inc(gout.id_rows, 1)
                    gather_back(gout, t)
                    corrections(gout, t, gout.corr, gout.corr_added, T * t + 1, False)
                pe.wait_ge(gout.loaded, 6 * NT)
                along_free(e2[:, 0:P], subm[:, 0:1]).then_inc(gout.id_rows, 1)
                gather_back(gout, NT - 1, one.gathered)
                corrections(one, 0, sem.corr, sem.y_sum, 0, True)
            with pe.Else():
                def fast_ids():
                    pe.wait_ge(one.slot_key, 1)
                    id_rows(one)

                def fast_att():
                    pe.wait_ge(one.att, 1)
                    att_rows(one)

                def fast_table():
                    row_table(0, 1, sem.row_table)

                def fast_gather():
                    pe.wait_ge(sem.row_pack, 1)
                    gather_back(one, 0)

                def correct(tiles):
                    return lambda: corrections(one, 0, sem.corr, sem.y_sum, 0, False, tiles)

                products(12, range(0, 6))
                fast_ids()
                biases()
                turn(one, 0)
                queries_keys()
                row_counts()
                products(12, range(6, 10))
                fast_att()
                products(12, range(10, T))
                tiles_with(range(13, 16), {
                    (13, 2): [fast_table],
                    (13, 15): [fast_gather],
                    (14, 5): [correct([0, 1])], (14, 8): [correct([2])], (14, 11): [correct([3])], (14, 14): [correct([4])],
                    (15, 2): [correct([5])], (15, 5): [correct([6])], (15, 9): [correct([7])], (15, 12): [correct([8])],
                })
                correct(range(9, T))()


def kernel(x, adj, L0_gnn_rel_pair_index, L0_gnn_Wq, L0_gnn_bq, L0_gnn_Wk, L0_gnn_bk):
    import numpy as np
    import concourse.bacc as bacc
    from concourse.bass_utils import run_bass_kernel_spmd as run

    nc = bacc.Bacc("TRN2", target_bir_lowering=False, num_devices=1)
    adj = np.ascontiguousarray(adj)
    n = adj.shape[0]
    t = n // 128
    blocks = np.ascontiguousarray(adj.reshape(t, 128, t, 128).transpose(0, 3, 2, 1)).reshape(t, 128, n)
    arrays = {
        "x": np.ascontiguousarray(x),
        "adj": adj,
        "adj_blocks": blocks,
        "adj_diag": np.ascontiguousarray(adj.diagonal().reshape(t, 128).T),
        "edges": np.ascontiguousarray(L0_gnn_rel_pair_index),
        "wq_t": np.ascontiguousarray(np.asarray(L0_gnn_Wq).T),
        "bq": np.ascontiguousarray(L0_gnn_bq),
        "wk_t": np.ascontiguousarray(np.asarray(L0_gnn_Wk).T),
        "bk": np.ascontiguousarray(L0_gnn_bk),
    }
    aps = [nc.dram_tensor(k, v.shape, mybir.dt.from_np(v.dtype), kind="ExternalInput").ap() for k, v in arrays.items()]
    out = nc.dram_tensor("out", arrays["x"].shape, mybir.dt.float32, kind="ExternalOutput").ap()
    graph_attention_norm(nc, *aps, out)
    r = run(nc, [arrays], core_ids=[0])
    return r.results[0]["out"]
```

```python
import concourse.bass as bass
from concourse import mybir
from contextlib import ExitStack
from collections import namedtuple


def graph_attention_norm(nc, x, adj, adj_blocks, adj_diag, edges, wq_t, bq, wk_t, bk, out):
    f32, f32r = mybir.dt.float32, mybir.dt.float32r
    bf16, i32, u32 = mybir.dt.bfloat16, mybir.dt.int32, mybir.dt.uint32
    ALU, ACT, AX = mybir.AluOpType, mybir.ActivationFunctionType, mybir.AxisListType

    N, H = x.shape
    E = edges.shape[0]
    HEADS = 8
    DK = H // HEADS
    P = 128
    T = N // P
    KC = H // P
    EP = 125
    EC = E // EP
    FIRST = 4
    ROUNDS = [1] * 6 + [2] * ((T - 6) // 2)
    STARTS = [sum(ROUNDS[:r]) for r in range(len(ROUNDS))]
    NR = len(ROUNDS)
    SUMMED = T - 4
    SAVED = T - 4
    WARM_UPS, WARM_COLS = 11, H // P
    DIAG_SCORE = 1e-7
    BIG = 3.0e38
    EPS = 1e-5
    NT = -(-E // P)
    OC = 10
    NOC = EC // OC
    LOT_ENDS = [OC * chunks for chunks in (2, 4, 6, 7, 8)]
    LOT_STARTS = [0] + LOT_ENDS[:-1]
    LOTS = len(LOT_ENDS)
    VECTOR_SUMS = (0, 1, 2)
    POOL_SUMS = [t for t in range(T - 1) if t not in VECTOR_SUMS]
    SCALED_X = (8, 10, 11, 12, 13, 14, T - 1)
    POOL_ROWS = (9, 11, 13, 14)
    GROUPS = [(0, 4), (4, 8), (8, 10), (10, 12), (12, 14), (14, 16)]

    ctx = ExitStack()
    with ctx:
        def sb(name, shape, dt):
            return ctx.enter_context(nc.sbuf_tensor(name, shape, dt))

        def pb(name, shape):
            return ctx.enter_context(nc.psum_tensor(name, shape, f32))

        def sems(prefix, names):
            return namedtuple("Semaphores", names)(*[ctx.enter_context(nc.semaphore(prefix + n)) for n in names.split()])

        sem = sems("", """x_r0 x_r1 x_r2 x_r3 x_r4 x_r5 x_r6 x_r7 x_r8 x_r9 x_r10 a_first0 a_first1 a_first2 a_first3 a_even a_odd
            edges_in diag_in weights_in biases_in adj_lot0 adj_lot1 adj_lot2 adj_lot3 adj_lot4 out_done
            x_high x_low masks_made products product_saved column_sums column_sums_pool column_tree
            edge_index edge_split edge_values edge_distinct const_vector const_pool const_eye
            live scan totals prefix prefix_copied live_count ranks counts counts_copied
            row_table off_diagonal row_max row_e0 row_ed diag_flag zero_count den_a den_b den_c row_r
            w_terms d_terms w_sum d_sum w_diag d_coef pack_ready row_parts row_pack corr
            weighted x_scaled x_scaled_act base base_vector y_sum stats aggr std rstd shift y_done y_done_pool""")
        slot_steps = """onehot_made onehot_used slots slots_copied slot_ids slot_index slot_sub slot_key
            x_sub x_obj sub_turned obj_turned sub_turned_sbuf obj_turned_sbuf
            q_done k_done q_sbuf qk_product qk_sum att"""
        pair_steps = """id_rows other_row id_flags flag_max att_rows_a att_rows_b masked_a masked_b score_max"""
        value_steps = """keep edge_max centred exps rowvals value_parts sub_tiles row_onehot onehot_wide table"""
        spread_steps = """row_onehot_t gathered shares coef_terms coef cx_high cx_low"""
        one = sems("one_", slot_steps + " " + pair_steps + " " + value_steps + " " + spread_steps)
        gen = sems("gen_", "prepared first_slot slot_shift stored")
        gpair = sems("pair_", "column_loaded row_loaded offset mask flag_join score_join valid_loaded kept")
        gval = sems("val_", "loaded table_added")
        gout = sems("spread_", spread_steps + " loaded id_rows x_obj corr corr_added")
        x_r = [sem.x_r0, sem.x_r1, sem.x_r2, sem.x_r3, sem.x_r4, sem.x_r5, sem.x_r6, sem.x_r7, sem.x_r8, sem.x_r9, sem.x_r10]
        a_first = [sem.a_first0, sem.a_first1, sem.a_first2, sem.a_first3]
        adj_lot = [sem.adj_lot0, sem.adj_lot1, sem.adj_lot2, sem.adj_lot3, sem.adj_lot4]
        a_par = [sem.a_even, sem.a_odd]

        xs = sb("xs", [P, T, H], f32)
        high_at = nc.sbuf_base
        xh = sb("xh", [P, T, H], f32r)
        xl = sb("xl", [P, T, H], f32r)
        prod = sb("prod", [P, SAVED, H], f32)
        blocks_at = nc.sbuf_base
        a = sb("a", [P, 2, N], f32)
        m_last = nc.alloc_sbuf_tensor_at("m_last", [P, N], f32r, offset=blocks_at + 4 * N)
        m = sb("m", [P, 3, N], f32r)
        weights_at = nc.sbuf_base
        w = sb("w", [P, 2, KC, H], f32)
        m_fourth = nc.alloc_sbuf_tensor_at("m_fourth", [P, N], f32r, offset=weights_at)
        onehot_at = nc.sbuf_base
        onehot_r = sb("onehot_r", [P, T, P], f32r)
        halves = nc.alloc_sbuf_tensor_at("halves", [P, N // 2], f32, offset=onehot_at)
        onehots_at = nc.sbuf_base
        oh = sb("oh", [EP, 2, OC, P], bf16)
        onehot_t = nc.alloc_sbuf_tensor_at("onehot_t", [P, T, P], bf16, offset=onehots_at)
        xsub = sb("xsub", [P, H], f32)
        xobj = sb("xobj", [P, H], f32)
        xsub_t = sb("xsub_t", [P, KC, P], f32)
        xobj_t = sb("xobj_t", [P, KC, P], f32)
        q_sb = xsub_t[:, :, :].rearrange("p k n -> p (k n)")
        qk = xsub[:, :]
        cs = sb("cs", [P, T, P], bf16)
        ed_in = sb("ed_in", [EP, EC, 2], i32)
        split = xsub[0:EP, 0:4 * EC].bitcast(i32)
        vals = sb("vals", [EP, EC, 5], bf16)
        idx = sb("idx", [EP, EC], i32)
        distinct = sb("distinct", [EP, EC], f32)
        adjv = sb("adjv", [EP, EC], f32)
        live = sb("live", [EP, EC], f32)
        incl = adjv
        rank = distinct
        tot = sb("tot", [EP, LOTS], bf16)
        base = sb("base", [EP, LOTS], f32)
        live_total = sb("live_total", [1, 1], i32)
        ones_f = sb("ones_f", [P, P], f32)
        ones_b = sb("ones_b", [P, P], bf16)
        ident = sb("ident", [P, P], f32)
        before = sb("before", [P, P], bf16)
        earlier = sb("earlier", [P, P], bf16)
        slot_no = sb("slot_no", [P, P], f32)
        col_no = sb("col_no", [P, P], f32)
        row_no = sb("row_no", [P, T], f32)
        tile_no = sb("tile_no", [P, T], f32)
        brow = nc.alloc_sbuf_tensor_at("brow", [1, 2, H], f32, offset=onehot_at + 4 * N // 2)
        diag = sb("diag", [P, T], f32)
        slot = sb("slot", [P, 5], f32)
        ids = sb("ids", [P, 2], f32)
        ids_i = sb("ids_i", [P, 2], i32)
        subm = sb("subm", [P, 1], f32)
        key = sb("key", [P, 1], f32)
        subt = sb("subt", [P, T], f32)
        nvalid = sb("nvalid", [P, 1], f32)
        att = sb("att", [P, HEADS], f32)
        mx = sb("mx", [P, HEADS], f32)
        flags = sb("flags", [P, 2], f32)
        keep = sb("keep", [P, 2], f32)
        cen = sb("cen", [P, HEADS], f32)
        pexp = sb("pexp", [P, HEADS], f32)
        rv = sb("rv", [P, 2 * HEADS + 1], f32)
        rv_parts = sb("rv_parts", [P, 3, 2 * HEADS + 1], bf16)
        share = sb("share", [P, HEADS + 1], f32)
        PK = 3 * (HEADS + 1)
        ct = sb("ct", [P, PK], f32)
        cf = sb("cf", [P, 1], f32)
        cnt = sb("cnt", [P, T], f32)
        wrow = sb("wrow", [P, T], f32)
        drow = sb("drow", [P, T], f32)
        eps = sb("eps", [P, 1], f32)
        dsc = sb("dsc", [P, 1], f32)
        w_flat = w[:, :, :, :].rearrange("p a k n -> p (a k n)")
        masked = w_flat[:, 0:HEADS * P].rearrange("p (h e) -> p h e", h=HEADS)
        rm = [w_flat[:, T * HEADS * i:T * HEADS * (i + 1)].rearrange("p (t h) -> p t h", t=T) for i in range(4)]
        pack_parts = w_flat[:, 3072:3288].bitcast(bf16).rearrange("p (t a h) -> p t a h", a=3, t=T)
        pack = a[:, 0, 0:T * (HEADS + 1)].rearrange("p (t h) -> p t h", t=T)
        stats = a[:, 0, 256:256 + 6 * T].rearrange("p (t c) -> p t c", t=T)
        mv = a[:, 0, 384:384 + 2 * T].rearrange("p (t c) -> p t c", t=T)
        onehot_b = a[:, 0, 1024:2048].bitcast(bf16).rearrange("p (t e) -> p t e", t=T)
        pen = a[:, 0, 640:768]
        same = a[:, 0, 768:1024].rearrange("p (a e) -> p a e", a=2)
        wd, sd, rs, sh = [a[:, 0, 512 + T * i:512 + T * (i + 1)] for i in range(4)]

        loop_space = nc.alloc_sbuf_tensor_at("slot_tiles", [P, 2 * T * H], f32, offset=high_at)
        taken = [0]

        def part(*dims):
            size = 1
            for n in dims:
                size *= n
            at = taken[0]
            taken[0] += size
            flat = loop_space[:, at:at + size]
            return flat if len(dims) == 1 else flat.rearrange("p (a b) -> p a b", a=dims[0])

        g_corr = part(T, H)
        g_sub, g_key, g_nvalid, g_valid = part(NT), part(NT), part(NT), part(NT)
        g_ids, g_keep = part(NT, 2), part(NT, 2)
        g_att, g_max = part(NT, HEADS), part(NT, HEADS)
        g_bias = part(2, H)[0:1]
        g_slot_no = part(P)
        g_firsts = part(NT)
        g_first, g_offset = part(1), part(1)
        g_diff = part(P)
        g_earlier = part(P)
        c_sub, c_key, c_max, c_flags = part(1), part(1), part(HEADS), part(2)
        g_table = part(T, 2 * HEADS + 1)

        def at(t):
            return bass.ds(t, 1)

        def weighted(t):
            return prod[:, t, :] if t < SAVED else w[:, 0, t - SAVED, :]

        def mask_of(t):
            if t in (3, T - 1):
                return m_fourth[:, :] if t == 3 else m_last[:, :]
            return m[:, t if t < 3 else (t - 4) % 3, :]

        a_round = a[:, :, :].rearrange("p b (c t n) -> p (b c) t n", c=2, t=FIRST)
        ROUND_MASKS = 2 * NR

        cx_parts = nc.alloc_sbuf_tensor_at("cx_parts", [P, 2, H], f32r, offset=weights_at + 4 * 2048)
        cx_high, cx_low = cx_parts[:, 0, :], cx_parts[:, 1, :]

        main = pb("main", [P, 4, H])
        e0, e1, e2, e3 = [pb(f"e{i}", [P, H]) for i in range(4)]
        RT = 2 * HEADS + 1
        table = e0[:, 32:32 + T * RT].rearrange("p (t c) -> p t c", t=T)
        counts = e1[:, 0:T]

        def corr_bank(t):
            return [e1, e3, e0, e2][t % 4]

        block = ctx.enter_context(nc.Block())

        @block.sync
        def _(sp):
            sp.dma_start(ed_in[:, :, :], edges.rearrange("(p c) t -> p c t", p=EP)).then_inc(sem.edges_in, 16)
            for r, (k0, n) in enumerate(zip(STARTS, ROUNDS)):
                sp.dma_start(xs[:, k0:k0 + n, :],
                             x[k0 * P:(k0 + n) * P, :].rearrange("(k p) c -> p k c", p=P)).then_inc(x_r[r], 16)
                if r >= 4:
                    sp.wait_ge(sem.masks_made, 2 * (r - 3))
                sp.dma_start(a_round[:, r % 4, :, 0:n * P],
                             adj_blocks[0:FIRST, :, k0 * P:(k0 + n) * P].rearrange("t p n -> p t n")).then_inc(a_first[r % 4], 16)
            for t in range(FIRST, T):
                if t < FIRST + 2:
                    sp.wait_ge(sem.masks_made, 2 * (1 + max(r for r in range(NR) if r % 4 // 2 == t % 2)))
                else:
                    sp.wait_ge(sem.masks_made, ROUND_MASKS + t - 5)
                sp.dma_start(a[:, t % 2, :], adj_blocks[t]).then_inc(a_par[t % 2], 16)
                if t == FIRST + 3:
                    sp.wait_ge(sem.products, FIRST)
                    sp.wait_ge(sem.column_sums, FIRST)
                    sp.dma_start(w[:, 0, :, :], wq_t.rearrange("(k p) n -> p k n", p=P)).then_inc(sem.weights_in, 16)
                    sp.dma_start(w[:, 1, :, :], wk_t.rearrange("(k p) n -> p k n", p=P)).then_inc(sem.weights_in, 16)
                    sp.dma_start(brow[:, 0, :], bq.rearrange("(a n) -> a n", a=1)).then_inc(sem.biases_in, 16)
                    sp.dma_start(brow[:, 1, :], bk.rearrange("(a n) -> a n", a=1)).then_inc(sem.biases_in, 16)
            for t in range(T):
                by_pool = len([u for u in POOL_ROWS if u <= t])
                if t in POOL_ROWS:
                    sp.wait_ge(sem.y_done_pool, by_pool)
                elif t < T - 1:
                    sp.wait_ge(sem.y_done, t + 1 - by_pool)
                else:
                    sp.wait_ge(sem.y_sum, T + 2)
                sp.dma_start(out[t * P:(t + 1) * P, :], xs[:, t, :]).then_inc(sem.out_done, 16)
            sp.wait_ge(sem.out_done, 16 * T)

        def general_branch(eng):
            eng.wait_ge(sem.live_count, 1)
            return eng.value_load(live_total[0:1, 0:1], min_val=0, max_val=E) > P

        @block.gpsimd
        def _(gp):
            g = nc.gpsimd
            g.memset(before[:, :], 1.0).then_inc(sem.const_pool, 1)
            g.memset(earlier[:, :], 1.0).then_inc(sem.const_pool, 1)
            g.memset(ident[:, :], 0.0).then_inc(sem.const_pool, 1)
            gp.wait_ge(sem.const_pool, 3)
            g.affine_select(out=before[:, :], in_=before[:, :], compare_op=ALU.is_gt, fill=0.0,
                            base=0, pattern=[[1, P]], channel_multiplier=-1).then_inc(sem.const_eye, 1)
            g.affine_select(out=earlier[:, :], in_=earlier[:, :], compare_op=ALU.is_gt, fill=0.0,
                            base=0, pattern=[[-1, P]], channel_multiplier=1).then_inc(sem.const_eye, 1)
            g.affine_select(out=ident[:, :], in_=ident[:, :], compare_op=ALU.not_equal, fill=1.0,
                            base=0, pattern=[[-1, P]], channel_multiplier=1).then_inc(sem.const_eye, 1)
            g.iota(slot_no[:, :], [[1, P]], 1, 0, allow_small_or_imprecise_dtypes=True).then_inc(sem.const_eye, 1)
            g.iota(col_no[:, :], [[1, P]], 0, 0, allow_small_or_imprecise_dtypes=True).then_inc(sem.const_eye, 1)
            g.iota(row_no[:, :], [[P, T]], 0, 1, allow_small_or_imprecise_dtypes=True).then_inc(sem.const_eye, 1)
            g.iota(tile_no[:, :], [[P, T]], 0, 0, allow_small_or_imprecise_dtypes=True).then_inc(sem.const_eye, 1)
            gp.wait_ge(sem.edge_index, 1)
            flat = adj.rearrange("i (j o) -> (i j) o", o=1)
            for c in range(EC):
                g.indirect_dma_start(adjv[:, c:c + 1], None, flat,
                                     bass.IndirectOffsetOnAxis(idx[:, c:c + 1].bitcast(u32), 0)).then_inc(adj_lot[[c < end for end in LOT_ENDS].index(True)], 16)

            def column_sum(n, steps):
                t = SUMMED + n
                for step in steps:
                    half = N // 2 ** (step + 1)
                    if step == 0:
                        gp.wait_ge(sem.masks_made, ROUND_MASKS + t - 3)
                        if n:
                            gp.wait_ge(sem.column_sums_pool, n)
                        src = mask_of(t).bitcast(f32)
                    else:
                        gp.wait_ge(sem.column_tree, 3 * n + step)
                        src = halves
                    if step < 3:
                        g.tensor_tensor(halves[:, 0:half], src[:, 0:half], src[:, half:2 * half], ALU.add).then_inc(sem.column_tree, 1)
                    else:
                        g.tensor_tensor(cs[:, t, :], src[:, 0:half], src[:, half:2 * half], ALU.add).then_inc(sem.column_sums_pool, 1)

            def gather_x(s, r, end, done):
                gp.wait_ge(s, r + 1)
                gp.nop(nofuse=True)
                g.indirect_dma_start([xsub, xobj][end][:, :], None, x,
                                     bass.IndirectOffsetOnAxis(ids_i[:, end:end + 1].bitcast(u32), 0)).then_inc(done, 16)

            column_sum(0, range(0, 2))
            gather_x(one.slot_index, 0, 0, one.x_sub)
            gather_x(one.slot_index, 0, 1, one.x_obj)
            column_sum(0, range(2, 4))
            for n in range(1, T - SUMMED):
                column_sum(n, range(4))
            with gp.If(general_branch(gp)):
                with gp.Fori(0, NT) as t:
                    gather_x(one.slot_index, t + 1, 0, one.x_sub)
                    gather_x(one.slot_index, t + 1, 1, one.x_obj)
                with gp.Fori(0, NT) as t:
                    gather_x(gout.loaded, 6 * t + 5, 1, gout.x_obj)
            gp.wait_ge(sem.d_coef, 1)
            for t in POOL_SUMS:
                if t in SCALED_X:
                    gp.wait_ge(sem.x_scaled_act, 1 + SCALED_X.index(t))
                else:
                    g.tensor_scalar(xs[:, t, :], xs[:, t, :], drow[:, t:t + 1], 1.0, ALU.mult, ALU.mult).then_inc(sem.x_scaled, 1)
                    gp.wait_ge(sem.x_scaled, len([u for u in POOL_SUMS if u <= t and u not in SCALED_X]))
                gp.wait_ge(sem.weighted, t + 1)
                g.tensor_tensor(xs[:, t, :], xs[:, t, :], weighted(t), ALU.add).then_inc(sem.base, 1)
            for t in POOL_ROWS:
                gp.wait_ge(sem.shift, 1 + [t < t1 for _, t1 in GROUPS].index(True))
                g.tensor_scalar(xs[:, t, :], xs[:, t, :], rs[:, t:t + 1], sh[:, t:t + 1], ALU.mult, ALU.add).then_inc(sem.y_done_pool, 1)

        @block.scalar
        def _(act):
            copy = nc.scalar.activation
            act.dma_start(diag[:, :], adj_diag).then_inc(sem.diag_in, 16)
            for r, (k0, n) in enumerate(zip(STARTS, ROUNDS)):
                act.wait_ge(x_r[r], 16)
                copy(xh[:, k0:k0 + n, :], xs[:, k0:k0 + n, :], ACT.Copy).then_inc(sem.x_high, 1)
            for t in range(SAVED):
                act.wait_ge(sem.products, t + 1)
                copy(prod[:, t, :], main[:, t % 4, :], ACT.Copy).then_inc(sem.product_saved, 1)

            def turned_and_q(s, r):
                act.wait_ge(s.sub_turned, r + 1)
                copy(xsub_t[:, :, :], e1[:, :].rearrange("p (k n) -> p k n", k=KC), ACT.Copy).then_inc(s.sub_turned_sbuf, 1)
                act.wait_ge(s.obj_turned, r + 1)
                copy(xobj_t[:, :, :], e0[:, :].rearrange("p (k n) -> p k n", k=KC), ACT.Copy).then_inc(s.obj_turned_sbuf, 1)
                act.wait_ge(s.q_done, r + 1)
                copy(q_sb, e3[:, :], ACT.Copy).then_inc(s.q_sbuf, 1)

            def edge_exp(s, r):
                act.wait_ge(s.centred, r + 1)
                copy(pexp[:, :], cen[:, :], ACT.Exp).then_inc(s.exps, 1)

            def onehot_wide(r, onehots):
                act.wait_ge(one.row_onehot, onehots)
                copy(onehot_r[:, :, :], onehot_b, ACT.Copy).then_inc(one.onehot_wide, 1)

            def row_exps():
                act.wait_ge(sem.row_max, 1)
                copy(rm[1], rm[0], ACT.Exp, scale=-1.0).then_inc(sem.row_e0, 1)
                copy(rm[2], rm[0], ACT.Exp, scale=-1.0, bias=dsc[:, 0:1]).then_inc(sem.row_ed, 1)

            def scale_and_normalise():
                act.wait_ge(sem.d_coef, 1)

                def scale(t):
                    if t >= SAVED:
                        act.wait_ge(sem.products, t + 1)
                    src = prod[:, t, :] if t < SAVED else main[:, t % 4, :]
                    copy(weighted(t), src, ACT.Copy, scale=wrow[:, t:t + 1]).then_inc(sem.weighted, 1)

                def x_scale(tiles):
                    for t in tiles:
                        copy(xs[:, t, :], xs[:, t, :], ACT.Copy, scale=drow[:, t:t + 1]).then_inc(sem.x_scaled_act, 1)

                def deviations(g):
                    t0, t1 = GROUPS[g]
                    act.wait_ge(sem.aggr, t1)
                    copy(sd[:, t0:t1], mv[:, t0:t1, 1], ACT.Sqrt, bias=eps[:, 0:1]).then_inc(sem.std, 1)

                def normalise(g, tiles):
                    act.wait_ge(sem.shift, g + 1)
                    for t in tiles:
                        if t < T - 1 and t not in POOL_ROWS:
                            copy(xs[:, t, :], xs[:, t, :], ACT.Identity, scale=rs[:, t:t + 1],
                                 bias=sh[:, t:t + 1]).then_inc(sem.y_done, 1)

                for t in range(T - 2):
                    scale(t)
                x_scale(SCALED_X[:4])
                deviations(0)
                x_scale(SCALED_X[4:])
                normalise(0, range(*GROUPS[0]))
                scale(T - 2)
                deviations(1)
                normalise(1, range(4, 7))
                deviations(2)
                normalise(1, range(7, 8))
                for g in range(2, len(GROUPS)):
                    if g > 2:
                        deviations(g)
                    normalise(g, range(*GROUPS[g]))

            turned_and_q(one, 0)
            with act.If(general_branch(act)):
                with act.Fori(0, NT) as t:
                    turned_and_q(one, t + 1)
                with act.Fori(0, NT) as t:
                    edge_exp(one, t)
                row_exps()
                with act.Fori(0, NT - 1) as t:
                    edge_exp(one, NT + t)
                    onehot_wide(t, NT + t + 2)
                edge_exp(one, 2 * NT - 1)
                onehot_wide(NT - 1, 2 * NT + 1)
                scale_and_normalise()
            with act.Else():
                edge_exp(one, 0)
                act.wait_ge(sem.column_sums_pool, T - SUMMED)
                onehot_wide(0, 1)
                row_exps()
                scale_and_normalise()

        @block.vector
        def _(dve):
            v = nc.vector
            v.memset(ones_b[:, :], 1.0).then_inc(sem.const_vector, 1)
            v.memset(oh[:, 0, 0:WARM_COLS, :], 1.0).then_inc(sem.const_vector, 1)
            v.memset(ones_f[:, :], 1.0).then_inc(sem.const_vector, 1)
            dve.wait_ge(sem.edges_in, 16)
            v.scalar_tensor_tensor(idx[:, :], ed_in[:, :, 0], float(N), ed_in[:, :, 1], ALU.mult, ALU.add).then_inc(sem.edge_index, 1)
            flat = ed_in[:, :, :].rearrange("p c t -> p (c t)")
            v.tensor_scalar(split[:, 0:2 * EC], flat, 4, None, ALU.logical_shift_right).then_inc(sem.edge_split, 1)
            v.tensor_scalar(split[:, 2 * EC:4 * EC], flat, 15, None, ALU.bitwise_and).then_inc(sem.edge_split, 1)
            dve.wait_ge(sem.edge_split, 2)
            v.tensor_copy(vals[:, :, 0:2], split[:, 0:2 * EC].rearrange("p (c t) -> p c t", t=2)).then_inc(sem.edge_values, 1)
            v.tensor_copy(vals[:, :, 2:4], split[:, 2 * EC:4 * EC].rearrange("p (c t) -> p c t", t=2)).then_inc(sem.edge_values, 1)
            v.memset(vals[:, :, 4:5], 1.0).then_inc(sem.edge_values, 1)
            v.tensor_tensor(distinct[:, :], ed_in[:, :, 0], ed_in[:, :, 1], ALU.not_equal).then_inc(sem.edge_distinct, 1)
            v.memset(eps[:, :], EPS).then_inc(sem.const_vector, 1)
            v.memset(dsc[:, :], DIAG_SCORE).then_inc(sem.const_vector, 1)
            for r, (k0, n) in enumerate(zip(STARTS, ROUNDS)):
                cols = slice(k0 * P, (k0 + n) * P)
                dve.wait_ge(sem.x_high, r + 1)
                v.tensor_tensor(xl[:, k0:k0 + n, :], xs[:, k0:k0 + n, :], xh[:, k0:k0 + n, :].bitcast(f32),
                                ALU.subtract).then_inc(sem.x_low, 1)
                dve.wait_ge(a_first[r % 4], 16 * (r // 4 + 1))
                v.tensor_scalar(m[:, :, cols], a_round[:, r % 4, 0:3, 0:n * P], 1.0, None, ALU.is_equal).then_inc(sem.masks_made, 1)
                v.tensor_scalar(m_fourth[:, cols], a_round[:, r % 4, 3, 0:n * P], 1.0, None, ALU.is_equal).then_inc(sem.masks_made, 1)

            def mask(t):
                dve.wait_ge(a_par[t % 2], 16 * (t // 2 - 1))
                if t < T - 1:
                    u = t - 4 if t < 7 else t - 3
                    dve.wait_ge(sem.products, u + 1)
                    dve.wait_ge(sem.column_sums, u + 1)
                v.tensor_scalar(mask_of(t), a[:, t % 2, :], 1.0, None, ALU.is_equal).then_inc(sem.masks_made, 1)

            def column_sum(t):
                dve.wait_ge(sem.masks_made, ROUND_MASKS if t < FIRST else ROUND_MASKS + t - 3)
                with nc.allow_low_precision(reason="counts up to 16 are exact in bfloat16"):
                    v.tensor_reduce(cs[:, t, :], mask_of(t).bitcast(f32).rearrange("p (j i) -> p i j", j=T),
                                    AX.X, ALU.add).then_inc(sem.column_sums, 1)

            def lot_scan(n):
                cols = slice(LOT_STARTS[n], LOT_ENDS[n])
                dve.wait_ge(adj_lot[n], 16 * (LOT_ENDS[n] - LOT_STARTS[n]))
                v.scalar_tensor_tensor(live[:, cols], adjv[:, cols], 1.0, distinct[:, cols], ALU.is_equal, ALU.mult).then_inc(sem.live, 1)
                dve.wait_ge(sem.live, n + 1)
                v.tensor_tensor_scan(incl[:, cols], ones_f[0:EP, 0:LOT_ENDS[n] - LOT_STARTS[n]], live[:, cols], 0.0, ALU.mult, ALU.add).then_inc(sem.scan, 1)
                dve.wait_ge(sem.scan, n + 1)
                v.tensor_copy(tot[:, n:n + 1], incl[:, LOT_ENDS[n] - 1:LOT_ENDS[n]]).then_inc(sem.totals, 1)

            def lot_ranks(n):
                cols = slice(LOT_STARTS[n], LOT_ENDS[n])
                dve.wait_ge(sem.prefix, n + 1)
                v.tensor_copy(base[:, n:n + 1], e1[0:EP, 0:1]).then_inc(sem.prefix_copied, 1)
                if n == LOTS - 1:
                    v.tensor_copy(live_total[:, :], e1[0:1, 1:2]).then_inc(sem.live_count, 1)
                dve.wait_ge(sem.prefix_copied, n + 1)
                v.scalar_tensor_tensor(rank[:, cols], incl[:, cols], base[:, n:n + 1], live[:, cols], ALU.add, ALU.mult).then_inc(sem.ranks, 1)
                dve.wait_ge(sem.ranks, n + 1)
                slot_onehots(one, 0, slot_no, range(LOT_STARTS[n] // OC, LOT_ENDS[n] // OC))

            def slot_onehots(s, r, numbers, lots=range(NOC)):
                for c in lots:
                    if c >= 2:
                        dve.wait_ge(s.onehot_used, (NOC - 1) * r + c - 1)
                    v.tensor_tensor(oh[:, c % 2, :, :],
                                    numbers[0:EP, :].unsqueeze(1).broadcast_to([EP, OC, P]),
                                    rank[:, c * OC:(c + 1) * OC].unsqueeze(2).broadcast_to([EP, OC, P]),
                                    ALU.is_equal).then_inc(s.onehot_made, 1)

            def slot_ids(s, r):
                dve.wait_ge(s.slots, r + 1)
                v.tensor_copy(slot[:, :], e0[:, 0:5]).then_inc(s.slots_copied, 1)
                dve.wait_ge(s.slots_copied, r + 1)
                v.scalar_tensor_tensor(ids[:, :], slot[:, 0:2], 16.0, slot[:, 2:4], ALU.mult, ALU.add).then_inc(s.slot_ids, 1)
                dve.wait_ge(s.slot_ids, r + 1)
                v.tensor_copy(ids_i[:, :], ids[:, :]).then_inc(s.slot_index, 1)
                v.scalar_tensor_tensor(subm[:, :], ids[:, 0:1], -1.0, slot[:, 4:5], ALU.add, ALU.add).then_inc(s.slot_sub, 1)
                v.scalar_tensor_tensor(key[:, :], ids[:, 0:1], float(N), ids[:, 1:2], ALU.mult, ALU.add).then_inc(s.slot_key, 1)
                v.tensor_scalar(nvalid[:, :], slot[:, 4:5], -1.0, None, ALU.mult).then_inc(s.slot_key, 1)

            def row_onehot(s, r):
                v.tensor_scalar(subt[:, :], tile_no[:, :], subm[:, 0:1], -1.0, ALU.subtract, ALU.mult).then_inc(s.sub_tiles, 1)
                dve.wait_ge(s.sub_tiles, r + 1)
                v.tensor_tensor(onehot_b, col_no[:, :].unsqueeze(1).broadcast_to([P, T, P]),
                                subt[:, :].unsqueeze(2).broadcast_to([P, T, P]), ALU.is_equal).then_inc(s.row_onehot, 1)

            def row_onehot_t(s, r, rows):
                dve.wait_ge(rows, r + 1)
                v.tensor_tensor(onehot_t[:, :, :], e2[:, 0:P].unsqueeze(1).broadcast_to([P, T, P]),
                                row_no[:, :].unsqueeze(2).broadcast_to([P, T, P]), ALU.is_equal).then_inc(s.row_onehot_t, 1)

            def edge_scores(s, r, k_bank):
                dve.wait_ge(s.q_sbuf, r + 1)
                dve.wait_ge(s.k_done, r + 1)
                v.tensor_tensor(qk, k_bank, q_sb, ALU.mult).then_inc(s.qk_product, 1)
                dve.wait_ge(s.qk_product, r + 1)
                v.tensor_reduce(att[:, :], qk.rearrange("p (h d) -> p h d", h=HEADS), AX.X, ALU.add).then_inc(s.qk_sum, 1)
                dve.wait_ge(s.qk_sum, r + 1)
                v.tensor_scalar(att[:, :], att[:, :], float(DK) ** -0.5, None, ALU.mult).then_inc(s.att, 1)

            def pair_flags(s, r, col_sub, col_key, mask):
                dve.wait_ge(s.id_rows, r + 1)
                v.tensor_scalar(pen, e2[:, 0:P], col_sub, -BIG, ALU.not_equal, ALU.mult).then_inc(s.other_row, 1)
                v.scalar_tensor_tensor(same[:, 0, :], e2[:, 0:P], col_sub, mask, ALU.is_equal, ALU.mult).then_inc(s.id_flags, 1)
                v.scalar_tensor_tensor(same[:, 1, :], e2[:, P:2 * P], col_key, mask, ALU.is_equal, ALU.mult).then_inc(s.id_flags, 1)
                dve.wait_ge(s.id_flags, 2 * r + 2)
                v.tensor_reduce(flags[:, :], same, AX.X, ALU.max).then_inc(s.flag_max, 1)

            def pair_max(s, r):
                penb = pen.unsqueeze(1).broadcast_to([P, 4, P])
                dve.wait_ge(s.other_row, r + 1)
                dve.wait_ge(s.att_rows_a, r + 1)
                v.tensor_tensor(masked[:, 0:4, :], e1[:, :].rearrange("p (h e) -> p h e", h=4), penb, ALU.add).then_inc(s.masked_a, 1)
                dve.wait_ge(s.att_rows_b, r + 1)
                v.tensor_tensor(masked[:, 4:8, :], e3[:, :].rearrange("p (h e) -> p h e", h=4), penb, ALU.add).then_inc(s.masked_b, 1)
                dve.wait_ge(s.masked_a, r + 1)
                dve.wait_ge(s.masked_b, r + 1)
                v.tensor_reduce(mx[:, :], masked, AX.X, ALU.max).then_inc(s.score_max, 1)

            def centre(s):
                v.tensor_tensor(cen[:, :], att[:, :], mx[:, :], ALU.subtract).then_inc(s.centred, 1)

            def row_values(s, r):
                v.tensor_scalar(rv[:, 0:HEADS], mx[:, :], keep[:, 0:1], None, ALU.mult).then_inc(s.rowvals, 1)
                v.tensor_copy(rv[:, 2 * HEADS:RT], keep[:, 1:2]).then_inc(s.rowvals, 1)
                dve.wait_ge(s.exps, r + 1)
                v.tensor_scalar(rv[:, HEADS:2 * HEADS], pexp[:, :], keep[:, 1:2], None, ALU.mult).then_inc(s.rowvals, 1)
                dve.wait_ge(s.rowvals, 3 * r + 3)
                for i in range(3):
                    v.tensor_copy(rv_parts[:, i, :], rv[:, :]).then_inc(s.value_parts, 1)
                    if i < 2:
                        dve.wait_ge(s.value_parts, 5 * r + 2 * i + 1)
                        v.tensor_tensor(rv[:, :], rv[:, :], rv_parts[:, i, :], ALU.subtract).then_inc(s.value_parts, 1)
                        dve.wait_ge(s.value_parts, 5 * r + 2 * i + 2)

            def edge_shares(s, r):
                v.tensor_scalar(share[:, 0:HEADS], pexp[:, :], keep[:, 1:2], 1.0 / HEADS, ALU.mult, ALU.mult).then_inc(s.shares, 1)
                v.tensor_scalar(share[:, HEADS:HEADS + 1], keep[:, 1:2], -1.0, None, ALU.mult).then_inc(s.shares, 1)

            def coefficients(s, r):
                dve.wait_ge(s.shares, 2 * r + 2)
                dve.wait_ge(s.gathered, r + 1)
                v.tensor_tensor(ct[:, :].rearrange("p (a h) -> p a h", a=3), e2[:, 0:PK].rearrange("p (a h) -> p a h", a=3),
                                share[:, :].unsqueeze(1).broadcast_to([P, 3, HEADS + 1]), ALU.mult).then_inc(s.coef_terms, 1)
                dve.wait_ge(s.coef_terms, r + 1)
                v.tensor_reduce(cf[:, :], ct[:, :], AX.X, ALU.add).then_inc(s.coef, 1)
                dve.wait_ge(s.coef, r + 1)
                v.tensor_scalar(cx_high, xobj[:, :], cf[:, 0:1], None, ALU.mult).then_inc(s.cx_high, 1)
                dve.wait_ge(s.cx_high, r + 1)
                v.scalar_tensor_tensor(cx_low, xobj[:, :], cf[:, 0:1], cx_high.bitcast(f32), ALU.mult, ALU.subtract).then_inc(s.cx_low, 1)

            def load_tile(s, t):
                v.tensor_copy(subm[:, :], g_sub[:, at(t)]).then_inc(s.loaded, 1)
                v.tensor_copy(att[:, :].unsqueeze(1), g_att[:, at(t), :]).then_inc(s.loaded, 1)
                v.tensor_copy(mx[:, :].unsqueeze(1), g_max[:, at(t), :]).then_inc(s.loaded, 1)
                v.tensor_copy(keep[:, :].unsqueeze(1), g_keep[:, at(t), :]).then_inc(s.loaded, 1)
                v.tensor_copy(key[:, :], g_key[:, at(t)]).then_inc(s.loaded, 1)

            def row_counts():
                dve.wait_ge(sem.counts, 1)
                v.tensor_copy(cnt[:, :], counts).then_inc(sem.counts_copied, 1)
                dve.wait_ge(sem.counts_copied, 1)
                v.tensor_tensor(cnt[:, :], cnt[:, :], diag[:, :], ALU.subtract).then_inc(sem.off_diagonal, 1)

            def softmax_rows():
                dve.wait_ge(sem.row_table, 1)
                v.tensor_scalar(rm[0], table[:, :, 0:HEADS], DIAG_SCORE, None, ALU.max).then_inc(sem.row_max, 1)
                dve.wait_ge(sem.off_diagonal, 1)
                v.tensor_tensor(cnt[:, :], cnt[:, :], table[:, :, 2 * HEADS], ALU.subtract).then_inc(sem.zero_count, 1)
                dve.wait_ge(sem.zero_count, 1)
                dve.wait_ge(sem.row_e0, 1)
                v.tensor_tensor(rm[3], rm[1], cnt[:, :].unsqueeze(2).broadcast_to([P, T, HEADS]), ALU.mult).then_inc(sem.den_a, 1)
                dve.wait_ge(sem.den_a, 1)
                v.tensor_tensor(rm[3], rm[3], table[:, :, HEADS:2 * HEADS], ALU.add).then_inc(sem.den_b, 1)
                dve.wait_ge(sem.den_b, 1)
                dve.wait_ge(sem.row_ed, 1)
                v.tensor_tensor(rm[3], rm[3], rm[2], ALU.add).then_inc(sem.den_c, 1)
                dve.wait_ge(sem.den_c, 1)
                v.reciprocal(pack[:, :, 0:HEADS], rm[3]).then_inc(sem.row_r, 1)
                dve.wait_ge(sem.row_r, 1)
                v.tensor_tensor(rm[1], rm[1], pack[:, :, 0:HEADS], ALU.mult).then_inc(sem.w_terms, 1)
                v.tensor_tensor(rm[2], rm[2], pack[:, :, 0:HEADS], ALU.mult).then_inc(sem.d_terms, 1)
                dve.wait_ge(sem.w_terms, 1)
                v.tensor_reduce(wrow[:, :], rm[1], AX.X, ALU.add).then_inc(sem.w_sum, 1)
                dve.wait_ge(sem.d_terms, 1)
                v.tensor_reduce(drow[:, :], rm[2], AX.X, ALU.add).then_inc(sem.d_sum, 1)
                dve.wait_ge(sem.w_sum, 1)
                v.tensor_scalar(wrow[:, :], wrow[:, :], 1.0 / HEADS, None, ALU.mult).then_inc(sem.w_sum, 1)
                dve.wait_ge(sem.w_sum, 2)
                v.tensor_copy(pack[:, :, HEADS], wrow[:, :]).then_inc(sem.pack_ready, 1)
                v.tensor_tensor(wd[:, :], wrow[:, :], diag[:, :], ALU.mult).then_inc(sem.w_diag, 1)
                dve.wait_ge(sem.pack_ready, 1)
                v.tensor_copy(pack_parts[:, :, 0, :], pack).then_inc(sem.row_parts, 1)
                dve.wait_ge(sem.d_sum, 1)
                dve.wait_ge(sem.w_diag, 1)
                v.scalar_tensor_tensor(drow[:, :], drow[:, :], 1.0 / HEADS, wd[:, :], ALU.mult, ALU.subtract).then_inc(sem.w_diag, 1)
                dve.wait_ge(sem.row_parts, 1)
                v.tensor_tensor(pack, pack, pack_parts[:, :, 0, :], ALU.subtract).then_inc(sem.row_parts, 1)
                dve.wait_ge(sem.w_diag, 2)
                v.tensor_scalar(drow[:, :], drow[:, :], 1.0, None, ALU.add).then_inc(sem.d_coef, 1)
                dve.wait_ge(sem.row_parts, 2)
                v.tensor_copy(pack_parts[:, :, 1, :], pack).then_inc(sem.row_parts, 1)
                dve.wait_ge(sem.row_parts, 3)
                v.tensor_tensor(pack, pack, pack_parts[:, :, 1, :], ALU.subtract).then_inc(sem.row_parts, 1)
                dve.wait_ge(sem.row_parts, 4)
                v.tensor_copy(pack_parts[:, :, 2, :], pack).then_inc(sem.row_pack, 1)

            def base_row(t):
                dve.wait_ge(sem.d_coef, 1)
                dve.wait_ge(sem.weighted, t + 1)
                v.scalar_tensor_tensor(xs[:, t, :], xs[:, t, :], drow[:, t:t + 1], weighted(t), ALU.mult, ALU.add).then_inc(sem.base_vector, 1)

            def group_scales(end):
                for g, (t0, t1) in enumerate(GROUPS):
                    if t1 == end:
                        sl = slice(t0, t1)
                        dve.wait_ge(sem.std, g + 1)
                        v.reciprocal(rs[:, sl], sd[:, sl]).then_inc(sem.rstd, 1)
                        dve.wait_ge(sem.rstd, g + 1)
                        v.scalar_tensor_tensor(sh[:, sl], mv[:, sl, 0], -1.0, rs[:, sl], ALU.mult, ALU.mult).then_inc(sem.shift, 1)

            def output_rows():
                for t in range(T + 2):
                    if t < T:
                        dve.wait_ge(sem.corr, t + 1)
                        if t == T - 1:
                            dve.wait_ge(sem.x_scaled_act, len(SCALED_X))
                        elif t in VECTOR_SUMS:
                            dve.wait_ge(sem.base_vector, 1 + VECTOR_SUMS.index(t))
                        else:
                            dve.wait_ge(sem.base, 1 + POOL_SUMS.index(t))
                        v.tensor_tensor(xs[:, t, :], xs[:, t, :], corr_bank(t)[:, :], ALU.add).then_inc(sem.y_sum, 1)
                        group_scales(t - 3)
                    if t == T:
                        dve.wait_ge(sem.y_sum, T)
                        dve.wait_ge(sem.products, T)
                        v.scalar_tensor_tensor(xs[:, T - 1, :], main[:, (T - 1) % 4, :], wrow[:, T - 1:T], xs[:, T - 1, :],
                                               ALU.mult, ALU.add).then_inc(sem.y_sum, 1)
                        group_scales(T - 2)
                        dve.wait_ge(sem.y_sum, T + 1)
                    if 1 <= t <= T:
                        dve.wait_ge(sem.y_sum, t)
                        v.bn_stats(stats[:, t - 1, :], xs[:, t - 1, :]).then_inc(sem.stats, 1)
                    if t >= 2:
                        dve.wait_ge(sem.stats, t - 1)
                        v.bn_aggr(mv[:, t - 2, :], stats[:, t - 2, :]).then_inc(sem.aggr, 1)
                group_scales(T)
                dve.wait_ge(sem.shift, len(GROUPS))
                v.tensor_scalar(xs[:, T - 1, :], xs[:, T - 1, :], rs[:, T - 1:T], sh[:, T - 1:T], ALU.mult, ALU.add).then_inc(sem.y_sum, 1)

            dve.wait_ge(sem.diag_in, 16)
            v.tensor_scalar(diag[:, :], diag[:, :], 1.0, None, ALU.is_equal).then_inc(sem.diag_flag, 1)
            dve.wait_ge(sem.diag_flag, 1)
            dve.wait_ge(sem.edge_distinct, 1)
            dve.wait_ge(sem.const_vector, 5)
            dve.wait_ge(sem.const_eye, 7)
            lot_scan(0)
            for t in range(FIRST):
                column_sum(t)
                if t < 3:
                    mask(t + 4)
                if t == 1:
                    lot_ranks(0)
            SCAN_BEFORE, SCAN_AFTER, RANK_AFTER = {12: 3}, {8: 1, 10: 2, 13: 4}, {9: 1, 11: 2, 12: 3}
            for t in range(7, 14):
                column_sum(t - 3)
                if t in SCAN_BEFORE:
                    lot_scan(SCAN_BEFORE[t])
                mask(t)
                if t in RANK_AFTER:
                    lot_ranks(RANK_AFTER[t])
                if t in SCAN_AFTER:
                    lot_scan(SCAN_AFTER[t])
            lot_ranks(LOTS - 1)
            slot_ids(one, 0)
            column_sum(11)
            mask(14)
            dve.wait_ge(one.slot_sub, 1)
            dve.wait_ge(sem.masks_made, ROUND_MASKS + T - 5)
            row_onehot(one, 0)
            mask(15)
            with dve.If(general_branch(dve)):
                edge_scores(one, 0, main[:, 3, :])
                row_counts()
                dve.wait_ge(sem.products, T)
                dve.wait_ge(sem.biases_in, 32)
                dve.wait_ge(one.att, 1)
                v.tensor_copy(g_bias, brow[:, :, :]).then_inc(gen.prepared, 1)
                v.memset(g_first, -float(P)).then_inc(gen.stored, 1)
                v.tensor_scalar(g_diff, col_no[:, :], row_no[:, 0:1], None, ALU.subtract).then_inc(gen.prepared, 1)
                dve.wait_ge(gen.prepared, 2)
                with dve.Fori(0, NT) as t:
                    dve.wait_ge(gen.stored, 7 * t + 1)
                    v.tensor_scalar(g_first, g_first, float(P), None, ALU.add).then_inc(gen.first_slot, 1)
                    dve.wait_ge(gen.first_slot, t + 1)
                    v.tensor_scalar(g_slot_no, slot_no[:, :], g_first, None, ALU.add).then_inc(gen.slot_shift, 1)
                    dve.wait_ge(gen.slot_shift, t + 1)
                    slot_onehots(one, t + 1, g_slot_no)
                    slot_ids(one, t + 1)
                    edge_scores(one, t + 1, e1[:, :])
                    dve.wait_ge(one.att, t + 2)
                    v.tensor_copy(g_att[:, at(t), :], att[:, :].unsqueeze(1)).then_inc(gen.stored, 1)
                    v.tensor_copy(g_sub[:, at(t)], subm[:, :]).then_inc(gen.stored, 1)
                    v.tensor_copy(g_key[:, at(t)], key[:, :]).then_inc(gen.stored, 1)
                    v.tensor_copy(g_nvalid[:, at(t)], nvalid[:, :]).then_inc(gen.stored, 1)
                    v.tensor_copy(g_valid[:, at(t)], slot[:, 4:5]).then_inc(gen.stored, 1)
                    v.tensor_copy(g_ids[:, at(t), :], ids[:, :].unsqueeze(1)).then_inc(gen.stored, 1)
                    v.tensor_copy(g_firsts[:, at(t)], g_first).then_inc(gen.stored, 1)
                v.memset(g_offset, 0.0).then_inc(gpair.score_join, 1)
                v.memset(c_flags, 0.0).then_inc(gpair.kept, 1)
                with dve.Fori(0, NT) as c:
                    dve.wait_ge(gen.stored, 7 * NT + 1)
                    dve.wait_ge(gpair.kept, 2 * c + 1)
                    v.tensor_copy(c_sub, g_sub[:, at(c)]).then_inc(gpair.column_loaded, 1)
                    v.tensor_copy(c_key, g_key[:, at(c)]).then_inc(gpair.column_loaded, 1)
                    v.memset(c_max, DIAG_SCORE).then_inc(gpair.column_loaded, 1)
                    v.memset(c_flags, 0.0).then_inc(gpair.column_loaded, 1)
                    with dve.Fori(0, NT) as r:
                        n = c * NT + r
                        dve.wait_ge(gpair.column_loaded, 4 * c + 4)
                        dve.wait_ge(gpair.score_join, n + 1)
                        v.tensor_copy(subm[:, :], g_sub[:, at(r)]).then_inc(gpair.row_loaded, 1)
                        v.tensor_copy(key[:, :], g_key[:, at(r)]).then_inc(gpair.row_loaded, 1)
                        v.tensor_copy(att[:, :].unsqueeze(1), g_att[:, at(r), :]).then_inc(gpair.row_loaded, 1)
                        v.tensor_tensor(g_offset, g_firsts[:, at(c)], g_firsts[:, at(r)], ALU.subtract).then_inc(gpair.offset, 1)
                        dve.wait_ge(gpair.offset, n + 1)
                        v.tensor_scalar(g_earlier, g_diff, g_offset, None, ALU.is_lt).then_inc(gpair.mask, 1)
                        dve.wait_ge(gpair.mask, n + 1)
                        pair_flags(one, n, c_sub, c_key, g_earlier)
                        dve.wait_ge(one.flag_max, n + 1)
                        v.tensor_tensor(c_flags, c_flags, flags[:, :], ALU.max).then_inc(gpair.flag_join, 1)
                        pair_max(one, n)
                        dve.wait_ge(one.score_max, n + 1)
                        v.tensor_tensor(c_max, c_max, mx[:, :], ALU.max).then_inc(gpair.score_join, 1)
                    dve.wait_ge(gpair.flag_join, NT * c + NT)
                    dve.wait_ge(gpair.score_join, NT * c + NT + 1)
                    v.tensor_copy(nvalid[:, :], g_nvalid[:, at(c)]).then_inc(gpair.valid_loaded, 1)
                    v.tensor_copy(slot[:, 4:5], g_valid[:, at(c)]).then_inc(gpair.valid_loaded, 1)
                    v.tensor_copy(g_max[:, at(c), :], c_max.unsqueeze(1)).then_inc(gpair.kept, 1)
                    dve.wait_ge(gpair.valid_loaded, 2 * c + 2)
                    v.tensor_scalar(g_keep[:, at(c), :], c_flags.unsqueeze(1), nvalid[:, 0:1], slot[:, 4:5],
                                    ALU.mult, ALU.add).then_inc(gpair.kept, 1)
                v.memset(g_table, 0.0).then_inc(gval.table_added, 1)
                with dve.Fori(0, NT) as t:
                    dve.wait_ge(gpair.kept, 2 * NT + 1)
                    dve.wait_ge(gval.table_added, t + 1)
                    load_tile(gval, t)
                    dve.wait_ge(gval.loaded, 5 * t + 5)
                    centre(one)
                    row_onehot(one, t + 1)
                    row_values(one, t)
                    dve.wait_ge(one.table, t + 1)
                    v.tensor_tensor(g_table, g_table, table, ALU.add).then_inc(gval.table_added, 1)
                softmax_rows()
                v.memset(g_corr, 0.0).then_inc(gout.corr_added, 1)

                def tile_state(t):
                    load_tile(gout, t)
                    v.tensor_copy(ids_i[:, :].unsqueeze(1), g_ids[:, at(t), :]).then_inc(gout.loaded, 1)
                    dve.wait_ge(gout.loaded, 6 * t + 6)
                    centre(one)
                    row_onehot(one, NT + 1 + t)
                    row_onehot_t(gout, t, gout.id_rows)

                with dve.Fori(0, NT - 1) as t:
                    dve.wait_ge(gout.corr_added, T * t + 1)
                    tile_state(t)
                    dve.wait_ge(one.exps, NT + t + 1)
                    dve.wait_ge(gout.x_obj, 16 * t + 16)
                    edge_shares(gout, t)
                    coefficients(gout, t)
                    for i in range(T):
                        dve.wait_ge(gout.corr, T * t + i + 1)
                        v.tensor_tensor(g_corr[:, i, :], g_corr[:, i, :], corr_bank(i)[:, :], ALU.add).then_inc(gout.corr_added, 1)
                dve.wait_ge(gout.corr_added, T * (NT - 1) + 1)
                tile_state(NT - 1)
                dve.wait_ge(one.exps, 2 * NT)
                dve.wait_ge(gout.x_obj, 16 * NT)
                edge_shares(one, 0)
                coefficients(one, 0)
                for t in VECTOR_SUMS:
                    base_row(t)
                output_rows()
            with dve.Else():
                dve.wait_ge(one.slot_key, 2)
                pair_flags(one, 0, subm[:, 0:1], key[:, 0:1], earlier[:, :])
                dve.wait_ge(one.flag_max, 1)
                v.tensor_scalar(keep[:, :], flags[:, :], nvalid[:, 0:1], slot[:, 4:5], ALU.mult, ALU.add).then_inc(one.keep, 1)
                row_onehot_t(one, 0, one.id_rows)
                edge_scores(one, 0, main[:, 3, :])
                pair_max(one, 0)
                dve.wait_ge(one.score_max, 1)
                v.tensor_scalar(mx[:, :], mx[:, :], DIAG_SCORE, None, ALU.max).then_inc(one.edge_max, 1)
                dve.wait_ge(one.edge_max, 1)
                dve.wait_ge(one.att, 1)
                centre(one)
                dve.wait_ge(one.keep, 1)
                row_values(one, 0)
                edge_shares(one, 0)
                row_counts()
                softmax_rows()
                base_row(0)
                base_row(1)
                coefficients(one, 0)
                base_row(2)
                output_rows()

        @block.tensor
        def _(pe):
            mm = nc.tensor.matmul

            def product(t, k):
                mask = mask_of(t)[:, k * P:(k + 1) * P]
                mm(main[:, t % 4, :], mask, xh[:, k, :], start=(k == 0), stop=False)
                last = mm(main[:, t % 4, :], mask, xl[:, k, :], start=False, stop=(k == T - 1))
                if k == T - 1:
                    last.then_inc(sem.products, 1)

            def prefix(n):
                pe.wait_ge(sem.totals, n + 1)
                if n:
                    pe.wait_ge(sem.prefix_copied, n)
                else:
                    pe.wait_ge(sem.const_eye, 7)
                mm(e1[0:EP, 0:1], before[0:EP, 0:EP], tot[:, n:n + 1], start=True, stop=(n == 0))
                for i in range(n):
                    last = mm(e1[0:EP, 0:1], ones_b[0:EP, 0:EP], tot[:, i:i + 1], start=False, stop=(i == n - 1))
                for i in range(LOTS if n == LOTS - 1 else 1):
                    last = mm(e1[0:1, 1:2], ones_b[0:EP, 0:1], tot[:, i:i + 1], start=(i == 0), stop=(i == (LOTS - 1 if n == LOTS - 1 else 0)))
                last.then_inc(sem.prefix, 1)

            def compact(s, r, lots=range(NOC)):
                for c in lots:
                    pe.wait_ge(s.onehot_made, NOC * r + c + 1)
                    for n in range(OC):
                        last = mm(e0[:, 0:5], oh[:, c % 2, n, :], vals[:, c * OC + n, :],
                                  start=(c == 0 and n == 0), stop=(c == NOC - 1 and n == OC - 1))
                    last.then_inc(s.onehot_used if c < NOC - 1 else s.slots, 1)

            def compact_lot(n):
                compact(one, 0, range(LOT_STARTS[n] // OC, LOT_ENDS[n] // OC))

            def turn(s, r):
                pe.wait_ge(s.x_sub, 16 * r + 16)
                for k in range(KC):
                    last = nc.tensor.transpose(e1[:, k * P:(k + 1) * P], xsub[:, k * P:(k + 1) * P], ident[:, :])
                last.then_inc(s.sub_turned, 1)
                pe.wait_ge(s.x_obj, 16 * r + 16)
                for k in range(KC):
                    last = nc.tensor.transpose(e0[:, k * P:(k + 1) * P], xobj[:, k * P:(k + 1) * P], ident[:, :])
                last.then_inc(s.obj_turned, 1)

            def bias_row(dst, bias):
                mm(dst, ones_f[0:1, :], bias, start=True, stop=False)

            def project(dst, src, weights, done):
                for k in range(KC):
                    last = mm(dst, src[:, k, :], weights[:, k, :], start=False, stop=(k == KC - 1))
                last.then_inc(done, 1)

            def along_free(dst, column):
                return mm(dst, column.broadcast_to([P, P]), ident[:, :], start=True, stop=True)

            def id_rows(s):
                along_free(e2[:, 0:P], subm[:, 0:1])
                along_free(e2[:, P:2 * P], key[:, 0:1]).then_inc(s.id_rows, 1)

            def att_rows(s):
                for dst, h0, done in ((e1, 0, s.att_rows_a), (e3, 4, s.att_rows_b)):
                    for h in range(4):
                        last = along_free(dst[:, h * P:(h + 1) * P], att[:, h0 + h:h0 + h + 1])
                    last.then_inc(done, 1)

            def row_counts():
                pe.wait_ge(sem.column_sums, SUMMED)
                pe.wait_ge(sem.column_sums_pool, T - SUMMED)
                for t in range(T):
                    last = mm(counts[:, t:t + 1], cs[:, t, :], ones_b[:, 0:1], start=True, stop=True)
                last.then_inc(sem.counts, 1)

            def row_table(r, onehots, done):
                pe.wait_ge(one.value_parts, 5 * r + 5)
                pe.wait_ge(one.row_onehot, onehots)
                for t in range(T):
                    for i in range(3):
                        last = mm(table[:, t, :], onehot_b[:, t, :], rv_parts[:, i, :], start=(i == 0), stop=(i == 2))
                last.then_inc(done, 1)

            def gather_back(s, r, done=None):
                pe.wait_ge(s.row_onehot_t, r + 1)
                for t in range(T):
                    last = mm(e2[:, 0:PK], onehot_t[:, t, :], pack_parts[:, t, :, :].rearrange("p a h -> p (a h)"),
                              start=(t == 0), stop=(t == T - 1))
                last.then_inc(done or s.gathered, 1)

            def corrections(s, r, done, used, first, general, tiles=range(T)):
                if tiles[0] == 0:
                    pe.wait_ge(one.onehot_wide, r + 1)
                    pe.wait_ge(s.cx_high, r + 1)
                    pe.wait_ge(s.cx_low, r + 1)
                for t in tiles:
                    if t >= 4:
                        pe.wait_ge(used, first + t - 3)
                    dst = corr_bank(t)
                    mm(dst[:, :], onehot_r[:, t, :], cx_high, start=True, stop=False)
                    last = mm(dst[:, :], onehot_r[:, t, :], cx_low, start=False, stop=not general)
                    if general:
                        last = mm(dst[:, :], ident[:, :], g_corr[:, t, :], start=False, stop=True)
                    last.then_inc(done, 1)

            def products(t, ks=range(T)):
                if ks[0] == 0:
                    pe.wait_ge(sem.masks_made, ROUND_MASKS + t - 3)
                    if t - 4 < SAVED:
                        pe.wait_ge(sem.product_saved, t - 3)
                for k in ks:
                    product(t, k)

            def query_bias():
                pe.wait_ge(sem.biases_in, 32)
                bias_row(e3[:, :], brow[:, 0, :])

            def key_bias():
                pe.wait_ge(sem.product_saved, SAVED)
                bias_row(main[:, 3, :], brow[:, 1, :])

            def queries_keys():
                pe.wait_ge(sem.weights_in, 32)
                pe.wait_ge(one.sub_turned_sbuf, 1)
                project(e3[:, :], xsub_t, w[:, 0, :, :], one.q_done)
                pe.wait_ge(one.obj_turned_sbuf, 1)
                project(main[:, 3, :], xobj_t, w[:, 1, :, :], one.k_done)

            def tiles_with(tiles, steps):
                for t in tiles:
                    at_k = [0] + sorted(k for tt, k in steps if tt == t and k) + [T]
                    for k0, k1 in zip(at_k, at_k[1:]):
                        for step in steps.get((t, k0), []):
                            step()
                        products(t, range(k0, k1))

            pe.wait_ge(sem.const_vector, 2)
            for _ in range(WARM_UPS):
                mm(e0[:, :], ones_b[0:EP, :], oh[:, 0, 0:WARM_COLS, :].rearrange("p a n -> p (a n)"), start=True, stop=True)
            for r, (k0, n) in enumerate(zip(STARTS, ROUNDS)):
                pe.wait_ge(sem.x_high, r + 1)
                pe.wait_ge(sem.x_low, r + 1)
                pe.wait_ge(sem.masks_made, 2 * r + 2)
                for t in range(FIRST):
                    for k in range(k0, k0 + n):
                        product(t, k)
            tiles_with(range(4, 12), {
                (4, 0): [lambda: prefix(0)], (5, 4): [lambda: compact_lot(0)],
                (7, 9): [lambda: prefix(1)], (8, 8): [lambda: compact_lot(1)],
                (9, 6): [lambda: prefix(2)], (9, 15): [lambda: compact_lot(2)],
                (10, 4): [lambda: prefix(3)], (11, 0): [lambda: compact_lot(3)],
                (11, 4): [lambda: prefix(4)], (11, 5): [query_bias], (11, 7): [lambda: compact_lot(4)],
            })
            with pe.If(general_branch(pe)):
                turn(one, 0)
                key_bias()
                queries_keys()
                pe.wait_ge(one.att, 1)
                tiles_with(range(12, 16), {})
                row_counts()
                pe.wait_ge(sem.counts_copied, 1)
                pe.wait_ge(gen.prepared, 2)
                with pe.Fori(0, NT) as t:
                    compact(one, t + 1)
                    turn(one, t + 1)
                    bias_row(e3[:, :], g_bias[:, 0, :])
                    pe.wait_ge(one.sub_turned_sbuf, t + 2)
                    project(e3[:, :], xsub_t, w[:, 0, :, :], one.q_done)
                    bias_row(e1[:, :], g_bias[:, 1, :])
                    pe.wait_ge(one.obj_turned_sbuf, t + 2)
                    project(e1[:, :], xobj_t, w[:, 1, :, :], one.k_done)
                with pe.Fori(0, NT) as c:
                    with pe.Fori(0, NT) as r:
                        n = c * NT + r
                        pe.wait_ge(gpair.row_loaded, 3 * n + 3)
                        id_rows(one)
                        att_rows(one)
                with pe.Fori(0, NT) as t:
                    row_table(t, t + 2, one.table)
                pe.wait_ge(gval.table_added, NT + 1)
                mm(e0[:, 32:32 + T * RT], ident[:, :], g_table.rearrange("p a b -> p (a b)"),
                   start=True, stop=True).then_inc(sem.row_table, 1)
                pe.wait_ge(sem.row_pack, 1)
                with pe.Fori(0, NT - 1) as t:
                    pe.wait_ge(gout.loaded, 6 * t + 6)
                    along_free(e2[:, 0:P], subm[:, 0:1]).then_inc(gout.id_rows, 1)
                    gather_back(gout, t)
                    corrections(gout, t, gout.corr, gout.corr_added, T * t + 1, False)
                pe.wait_ge(gout.loaded, 6 * NT)
                along_free(e2[:, 0:P], subm[:, 0:1]).then_inc(gout.id_rows, 1)
                gather_back(gout, NT - 1, one.gathered)
                pe.wait_ge(one.onehot_wide, NT)
                corrections(one, 0, sem.corr, sem.y_sum, 0, True)
            with pe.Else():
                def fast_ids():
                    pe.wait_ge(one.slot_key, 1)
                    id_rows(one)

                def fast_att():
                    pe.wait_ge(one.att, 1)
                    att_rows(one)

                def fast_counts():
                    pe.wait_ge(one.masked_a, 1)
                    row_counts()

                def fast_table():
                    row_table(0, 1, sem.row_table)

                def fast_gather():
                    pe.wait_ge(sem.row_pack, 1)
                    gather_back(one, 0)

                def correct(tiles):
                    return lambda: corrections(one, 0, sem.corr, sem.y_sum, 0, False, tiles)

                fast_ids()
                products(12, range(0, 1))
                turn(one, 0)
                key_bias()
                queries_keys()
                products(12, range(1, 6))
                fast_att()
                products(12, range(6, 14))
                fast_counts()
                products(12, range(14, 15))
                fast_table()
                products(12, range(15, T))
                tiles_with(range(13, 16), {
                    (13, 12): [fast_gather],
                    (14, 2): [correct([0, 1])], (14, 4): [correct([2])], (14, 6): [correct([3])],
                    (14, 8): [correct([4])], (14, 10): [correct([5])], (14, 12): [correct([6])], (14, 14): [correct([7])],
                    (15, 0): [correct([8])], (15, 2): [correct([9])], (15, 4): [correct([10])], (15, 6): [correct([11])],
                    (15, 8): [correct([12])], (15, 10): [correct([13])], (15, 12): [correct([14])], (15, 14): [correct([15])],
                })


def kernel(x, adj, L0_gnn_rel_pair_index, L0_gnn_Wq, L0_gnn_bq, L0_gnn_Wk, L0_gnn_bk):
    import numpy as np
    import concourse.bacc as bacc
    from concourse.bass_utils import run_bass_kernel_spmd as run

    nc = bacc.Bacc("TRN2", target_bir_lowering=False, num_devices=1)
    adj = np.ascontiguousarray(adj)
    n = adj.shape[0]
    t = n // 128
    blocks = np.ascontiguousarray(adj.reshape(t, 128, t, 128).transpose(0, 3, 2, 1)).reshape(t, 128, n)
    arrays = {
        "x": np.ascontiguousarray(x),
        "adj": adj,
        "adj_blocks": blocks,
        "adj_diag": np.ascontiguousarray(adj.diagonal().reshape(t, 128).T),
        "edges": np.ascontiguousarray(L0_gnn_rel_pair_index),
        "wq_t": np.ascontiguousarray(np.asarray(L0_gnn_Wq).T),
        "bq": np.ascontiguousarray(L0_gnn_bq),
        "wk_t": np.ascontiguousarray(np.asarray(L0_gnn_Wk).T),
        "bk": np.ascontiguousarray(L0_gnn_bk),
    }
    aps = [nc.dram_tensor(k, v.shape, mybir.dt.from_np(v.dtype), kind="ExternalInput").ap() for k, v in arrays.items()]
    out = nc.dram_tensor("out", arrays["x"].shape, mybir.dt.float32, kind="ExternalOutput").ap()
    graph_attention_norm(nc, *aps, out)
    r = run(nc, [arrays], core_ids=[0])
    return r.results[0]["out"]
```
